# Optimizing a Trainium2 kernel written in Bass

```python
import numpy as np
import jax
import jax.numpy as jnp

def _softmax(x, axis=-1):
    return jax.nn.softmax(x, axis=axis)

def _gelu(x):
    return jax.nn.gelu(x, approximate=True)

def _silu(x):
    return jax.nn.silu(x)

def _sigmoid(x):
    return jax.nn.sigmoid(x)

def _layernorm(x, axis=-1, eps=1e-05):
    m = jnp.mean(x, axis=axis, keepdims=True)
    v = jnp.var(x, axis=axis, keepdims=True)
    return (x - m) / jnp.sqrt(v + eps)

def _scatter_add(tgt, idx, src, axis=0):
    return tgt.at[idx].add(src)

def _segment_sum(src, seg, n):
    return jax.ops.segment_sum(src, seg, n)
kernel_name = 'mk_audio_tower_d1_tok_audfeat256_r4_fd2af5'

def setup_inputs(seed: int=0):
    np.random.seed(seed)
    _w = jnp.asarray

    def _rec_inputs():
        import jax
        import jax.numpy as jnp
        _rk = jax.random.key(seed)
        x = -5.07413e-05 + 0.999912 * jax.random.normal(jax.random.fold_in(_rk, 1), (32, 750, 64), jnp.float32)
        return x
    x = _rec_inputs()

    def _L0_tok_setup():
        import jax, jax.numpy as jnp
        from jax import lax
        import numpy as np
        B, T, C, K, STRIDE = (16, 4000, 64, 5, 2)
        EPS = 0.001
        key = jax.random.key(seed)
        k0, k1, k2, k3 = jax.random.split(key, 4)
        x = jax.random.normal(k0, (B, T, C), dtype=jnp.float32)
        w = jax.random.normal(k1, (K, 1, C), dtype=jnp.float32) * 0.1
        b = jax.random.normal(k2, (C,), dtype=jnp.float32) * 0.01
        gamma = jnp.ones((C,), dtype=jnp.float32)
        beta = jnp.zeros((C,), dtype=jnp.float32)
        alpha = jnp.full((C,), 0.25, dtype=jnp.float32) + 0.01 * jax.random.normal(k3, (C,), dtype=jnp.float32)
        return {'x': x, 'w': w, 'b': b, 'gamma': gamma, 'beta': beta, 'alpha': alpha}
    _L0_tok_all = _L0_tok_setup()
    _L0_tok_in = {k: v for k, v in _L0_tok_all.items() if k in ('w', 'b', 'gamma', 'beta', 'alpha')}
    del _L0_tok_all

    def _L0_attn_setup():
        import jax, jax.numpy as jnp
        import numpy as np
        D_MODEL = 64
        D_STATE = 16
        D_CONV = 4
        EXPAND = 2
        D_INNER = EXPAND * D_MODEL
        DT_RANK = 16
        BATCH = 8
        SEQLEN = 1024

        def _mamba_block(u, in_w, conv_w, conv_b, xproj_w, dt_w, dt_b, A_log, D, out_w):
            Bsz, L, _ = u.shape
            d_in = in_w.shape[0] // 2
            N = A_log.shape[1]
            dt_rank = dt_w.shape[1]
            xz = u @ in_w.T
            x, z = (xz[..., :d_in], xz[..., d_in:])
            xc = x.transpose(0, 2, 1)
            k = conv_w[:, None, :]
            xc = jax.lax.conv_general_dilated(xc, k, window_strides=(1,), padding=[(D_CONV - 1, 0)], dimension_numbers=('NCH', 'OIH', 'NCH'), feature_group_count=d_in)
            x = jax.nn.silu(xc.transpose(0, 2, 1) + conv_b)
            dbl = x @ xproj_w.T
            dt = dbl[..., :dt_rank]
            Bm = dbl[..., dt_rank:dt_rank + N]
            Cm = dbl[..., dt_rank + N:]
            delta = jax.nn.softplus(dt @ dt_w.T + dt_b)
            A = -jnp.exp(A_log)

            def step(h, inp):
                u_t, dt_t, B_t, C_t = inp
                h = jnp.exp(dt_t[:, :, None] * A) * h + (dt_t * u_t)[:, :, None] * B_t[:, None, :]
                y = jnp.einsum('bdn,bn->bd', h, C_t)
                return (h, y)
            h0 = jnp.zeros((Bsz, d_in, N), dtype=u.dtype)
            _, ys = jax.lax.scan(step, h0, (x.transpose(1, 0, 2), delta.transpose(1, 0, 2), Bm.transpose(1, 0, 2), Cm.transpose(1, 0, 2)))
            y = ys.transpose(1, 0, 2) + x * D
            y = y * jax.nn.silu(z)
            return y @ out_w.T
        key = jax.random.key(seed)
        ks = jax.random.split(key, 16)
        w = lambda k, shape, s=0.02: jax.random.normal(k, shape, jnp.float32) * s
        inp = {'hidden_states': jax.random.normal(ks[0], (BATCH, SEQLEN, D_MODEL), jnp.float32)}
        A_log_init = jnp.tile(jnp.log(jnp.arange(1.0, D_STATE + 1.0, dtype=jnp.float32))[None, :], (D_INNER, 1))
        i = 1
        for p in ('f', 'b'):
            inp[p + '_in_w'] = w(ks[i], (2 * D_INNER, D_MODEL))
            i += 1
            inp[p + '_conv_w'] = w(ks[i], (D_INNER, D_CONV), 0.1)
            i += 1
            inp[p + '_conv_b'] = jnp.zeros((D_INNER,), jnp.float32)
            inp[p + '_xproj_w'] = w(ks[i], (DT_RANK + 2 * D_STATE, D_INNER))
            i += 1
            inp[p + '_dt_w'] = w(ks[i], (D_INNER, DT_RANK), 0.1)
            i += 1
            inp[p + '_dt_b'] = jnp.full((D_INNER,), -2.0, jnp.float32)
            inp[p + '_A_log'] = A_log_init
            inp[p + '_D'] = jnp.ones((D_INNER,), jnp.float32)
            inp[p + '_out_w'] = w(ks[i], (D_MODEL, D_INNER))
            i += 1
        return inp
    _L0_attn_all = _L0_attn_setup()
    _L0_attn_in = {k: v for k, v in _L0_attn_all.items() if k in ('f_in_w', 'f_conv_w', 'f_conv_b', 'f_xproj_w', 'f_dt_w', 'f_dt_b', 'f_A_log', 'f_D', 'f_out_w', 'b_in_w', 'b_conv_w', 'b_conv_b', 'b_xproj_w', 'b_dt_w', 'b_dt_b', 'b_A_log', 'b_D', 'b_out_w')}
    del _L0_attn_all

    def _L0_ffn_setup():
        import jax, jax.numpy as jnp
        import numpy as np
        B, T, D, H, E = (16, 1024, 64, 128, 8)
        key = jax.random.key(seed)
        ks = jax.random.split(key, 5)
        x = jax.random.normal(ks[0], (B, T, D), dtype=jnp.float32)
        gate_w = jax.random.normal(ks[1], (D, E), dtype=jnp.float32) * 0.02
        gate_b = jnp.zeros((E,), dtype=jnp.float32)
        W1 = jax.random.normal(ks[2], (E, D, H), dtype=jnp.float32) * 0.02
        b1 = jnp.zeros((E, H), dtype=jnp.float32)
        W2 = jax.random.normal(ks[3], (E, H, D), dtype=jnp.float32) * 0.02
        b2 = jnp.zeros((E, D), dtype=jnp.float32)
        return {'x': x, 'gate_w': gate_w, 'gate_b': gate_b, 'W1': W1, 'b1': b1, 'W2': W2, 'b2': b2}
    _L0_ffn_all = _L0_ffn_setup()
    _L0_ffn_in = {k: v for k, v in _L0_ffn_all.items() if k in ('gate_w', 'gate_b', 'W1', 'b1', 'W2', 'b2')}
    del _L0_ffn_all
    return {'x': x, 'L0_tok_w': _L0_tok_in['w'], 'L0_tok_b': _L0_tok_in['b'], 'L0_tok_gamma': _L0_tok_in['gamma'], 'L0_tok_beta': _L0_tok_in['beta'], 'L0_tok_alpha': _L0_tok_in['alpha'], 'L0_attn_f_in_w': _L0_attn_in['f_in_w'], 'L0_attn_f_conv_w': _L0_attn_in['f_conv_w'], 'L0_attn_f_conv_b': _L0_attn_in['f_conv_b'], 'L0_attn_f_xproj_w': _L0_attn_in['f_xproj_w'], 'L0_attn_f_dt_w': _L0_attn_in['f_dt_w'], 'L0_attn_f_dt_b': _L0_attn_in['f_dt_b'], 'L0_attn_f_A_log': _L0_attn_in['f_A_log'], 'L0_attn_f_D': _L0_attn_in['f_D'], 'L0_attn_f_out_w': _L0_attn_in['f_out_w'], 'L0_attn_b_in_w': _L0_attn_in['b_in_w'], 'L0_attn_b_conv_w': _L0_attn_in['b_conv_w'], 'L0_attn_b_conv_b': _L0_attn_in['b_conv_b'], 'L0_attn_b_xproj_w': _L0_attn_in['b_xproj_w'], 'L0_attn_b_dt_w': _L0_attn_in['b_dt_w'], 'L0_attn_b_dt_b': _L0_attn_in['b_dt_b'], 'L0_attn_b_A_log': _L0_attn_in['b_A_log'], 'L0_attn_b_D': _L0_attn_in['b_D'], 'L0_attn_b_out_w': _L0_attn_in['b_out_w'], 'L0_ffn_gate_w': _L0_ffn_in['gate_w'], 'L0_ffn_gate_b': _L0_ffn_in['gate_b'], 'L0_ffn_W1': _L0_ffn_in['W1'], 'L0_ffn_b1': _L0_ffn_in['b1'], 'L0_ffn_W2': _L0_ffn_in['W2'], 'L0_ffn_b2': _L0_ffn_in['b2']}

def reference(x, L0_tok_w, L0_tok_b, L0_tok_gamma, L0_tok_beta, L0_tok_alpha, L0_attn_f_in_w, L0_attn_f_conv_w, L0_attn_f_conv_b, L0_attn_f_xproj_w, L0_attn_f_dt_w, L0_attn_f_dt_b, L0_attn_f_A_log, L0_attn_f_D, L0_attn_f_out_w, L0_attn_b_in_w, L0_attn_b_conv_w, L0_attn_b_conv_b, L0_attn_b_xproj_w, L0_attn_b_dt_w, L0_attn_b_dt_b, L0_attn_b_A_log, L0_attn_b_D, L0_attn_b_out_w, L0_ffn_gate_w, L0_ffn_gate_b, L0_ffn_W1, L0_ffn_b1, L0_ffn_W2, L0_ffn_b2):
    import jax
    import jax.numpy as jnp

    def _L0_tok_ref(x, w, b, gamma, beta, alpha):
        import jax, jax.numpy as jnp
        from jax import lax
        import numpy as np
        B, T, C, K, STRIDE = (16, 4000, 64, 5, 2)
        EPS = 0.001
        y = lax.conv_general_dilated(x, w, window_strides=(STRIDE,), padding='SAME', dimension_numbers=('NWC', 'WIO', 'NWC'), feature_group_count=C) + b
        mean = jnp.mean(y, axis=(1, 2), keepdims=True)
        var = jnp.var(y, axis=(1, 2), keepdims=True)
        yn = (y - mean) * lax.rsqrt(var + EPS) * gamma + beta
        return jnp.where(yn > 0, yn, alpha * yn)

    def _L0_attn_ref(hidden_states, f_in_w, f_conv_w, f_conv_b, f_xproj_w, f_dt_w, f_dt_b, f_A_log, f_D, f_out_w, b_in_w, b_conv_w, b_conv_b, b_xproj_w, b_dt_w, b_dt_b, b_A_log, b_D, b_out_w):
        import jax, jax.numpy as jnp
        import numpy as np
        D_MODEL = 64
        D_STATE = 16
        D_CONV = 4
        EXPAND = 2
        D_INNER = EXPAND * D_MODEL
        DT_RANK = 16
        BATCH = 8
        SEQLEN = 1024

        def _mamba_block(u, in_w, conv_w, conv_b, xproj_w, dt_w, dt_b, A_log, D, out_w):
            Bsz, L, _ = u.shape
            d_in = in_w.shape[0] // 2
            N = A_log.shape[1]
            dt_rank = dt_w.shape[1]
            xz = u @ in_w.T
            x, z = (xz[..., :d_in], xz[..., d_in:])
            xc = x.transpose(0, 2, 1)
            k = conv_w[:, None, :]
            xc = jax.lax.conv_general_dilated(xc, k, window_strides=(1,), padding=[(D_CONV - 1, 0)], dimension_numbers=('NCH', 'OIH', 'NCH'), feature_group_count=d_in)
            x = jax.nn.silu(xc.transpose(0, 2, 1) + conv_b)
            dbl = x @ xproj_w.T
            dt = dbl[..., :dt_rank]
            Bm = dbl[..., dt_rank:dt_rank + N]
            Cm = dbl[..., dt_rank + N:]
            delta = jax.nn.softplus(dt @ dt_w.T + dt_b)
            A = -jnp.exp(A_log)

            def step(h, inp):
                u_t, dt_t, B_t, C_t = inp
                h = jnp.exp(dt_t[:, :, None] * A) * h + (dt_t * u_t)[:, :, None] * B_t[:, None, :]
                y = jnp.einsum('bdn,bn->bd', h, C_t)
                return (h, y)
            h0 = jnp.zeros((Bsz, d_in, N), dtype=u.dtype)
            _, ys = jax.lax.scan(step, h0, (x.transpose(1, 0, 2), delta.transpose(1, 0, 2), Bm.transpose(1, 0, 2), Cm.transpose(1, 0, 2)))
            y = ys.transpose(1, 0, 2) + x * D
            y = y * jax.nn.silu(z)
            return y @ out_w.T
        fwd = _mamba_block(hidden_states, f_in_w, f_conv_w, f_conv_b, f_xproj_w, f_dt_w, f_dt_b, f_A_log, f_D, f_out_w)
        rev = hidden_states[:, ::-1, :]
        bwd = _mamba_block(rev, b_in_w, b_conv_w, b_conv_b, b_xproj_w, b_dt_w, b_dt_b, b_A_log, b_D, b_out_w)[:, ::-1, :]
        return (fwd + bwd) * 0.5

    def _L0_ffn_ref(x, gate_w, gate_b, W1, b1, W2, b2):
        import jax, jax.numpy as jnp
        import numpy as np
        B, T, D, H, E = (16, 1024, 64, 128, 8)
        Bb, Tt, Dd = x.shape
        Ee = gate_w.shape[1]
        xf = x.reshape(-1, Dd)
        N = xf.shape[0]
        logits = xf @ gate_w + gate_b
        probs = jax.nn.softmax(logits, axis=-1)
        top2_vals, top2_idx = jax.lax.top_k(probs, 2)
        cw = jnp.zeros((N, Ee), dtype=xf.dtype).at[jnp.arange(N)[:, None], top2_idx].add(top2_vals)

        def step(acc, params):
            w1, bb1, w2, bb2, we = params
            h = jax.nn.gelu(xf @ w1 + bb1, approximate=False)
            y = h @ w2 + bb2
            return (acc + we[:, None] * y, None)
        out, _ = jax.lax.scan(step, jnp.zeros_like(xf), (W1, b1, W2, b2, cw.T))
        return out.reshape(Bb, Tt, Dd)
    h = _L0_tok_ref(x, L0_tok_w, L0_tok_b, L0_tok_gamma, L0_tok_beta, L0_tok_alpha)
    h = h + _L0_attn_ref(_layernorm(h, axis=-1), L0_attn_f_in_w, L0_attn_f_conv_w, L0_attn_f_conv_b, L0_attn_f_xproj_w, L0_attn_f_dt_w, L0_attn_f_dt_b, L0_attn_f_A_log, L0_attn_f_D, L0_attn_f_out_w, L0_attn_b_in_w, L0_attn_b_conv_w, L0_attn_b_conv_b, L0_attn_b_xproj_w, L0_attn_b_dt_w, L0_attn_b_dt_b, L0_attn_b_A_log, L0_attn_b_D, L0_attn_b_out_w)
    h = h + _L0_ffn_ref(_layernorm(h, axis=-1), L0_ffn_gate_w, L0_ffn_gate_b, L0_ffn_W1, L0_ffn_b1, L0_ffn_W2, L0_ffn_b2)
    return h

_drawn_inputs = setup_inputs


def setup_inputs(seed=0):
    import zlib

    import numpy as np

    out = dict(_drawn_inputs(seed))
    spreads = {'L0_tok_gamma': (1.0, 0.2),
     'L0_tok_beta': (0.0, 0.1),
     'L0_attn_f_conv_b': (0.0, 0.8),
     'L0_attn_f_dt_b': (-2.0, 0.6),
     'L0_attn_f_D': (1.0, 0.6),
     'L0_attn_b_conv_b': (0.0, 0.8),
     'L0_attn_b_dt_b': (-2.0, 0.6),
     'L0_attn_b_D': (1.0, 0.6),
     'L0_ffn_gate_b': (0.0, 2.0),
     'L0_ffn_b1': (0.0, 2.0),
     'L0_ffn_b2': (0.0, 2.0)}
    factors = {'L0_tok_alpha': 4.521,
     'L0_attn_f_in_w': 8.0,
     'L0_attn_f_conv_w': 8.0,
     'L0_attn_f_xproj_w': 8.0,
     'L0_attn_f_dt_w': 8.0,
     'L0_attn_f_A_log': 8.0,
     'L0_attn_f_out_w': 8.0,
     'L0_attn_b_in_w': 8.0,
     'L0_attn_b_conv_w': 8.0,
     'L0_attn_b_xproj_w': 8.0,
     'L0_attn_b_dt_w': 8.0,
     'L0_attn_b_A_log': 8.0,
     'L0_attn_b_out_w': 8.0,
     'L0_ffn_W1': 64.0,
     'L0_ffn_W2': 64.0,
     'L0_ffn_gate_w': 8.0}
    for name, (base, spread) in spreads.items():
        noise = np.random.default_rng([zlib.crc32(name.encode()), seed]).standard_normal(out[name].shape)
        drawn = base * np.exp(spread * noise) if base else spread * noise
        out[name] = jnp.asarray(drawn.astype(out[name].dtype))
    for name, factor in factors.items():
        out[name] = (out[name] * factor).astype(out[name].dtype)
    return out
```

```python
from contextlib import ExitStack

import concourse.bass as bass
from concourse import mybir

ALU = mybir.AluOpType
ACT = mybir.ActivationFunctionType
AX = mybir.AxisListType
F32 = mybir.dt.float32

P = 128
CLIPS, TOKENS, CH = 32, 375, 64
PAIRS = CLIPS // 2
TAPS = 5
DIN, NSTATE, RANK, CTAPS = 128, 16, 16, 4
ND, NN = 32, 4
DG, NG = DIN // ND, NSTATE // NN
UNITS = 4
STEPS = UNITS * DG
EXPERTS, HID = 8, 128
AHEAD = 2
LOG_MARGIN = 2.0 ** -23
CHUNKS, CT = 3, 125

COLS = {}
for _name, _n in (("tok_w", TAPS), ("tok_b", 1), ("gamma", 1), ("beta", 1), ("alpha", 1), ("conv_b", 2), ("dt_b", 2),
                  ("D", 2), ("a_log", 2 * DG * NG), ("b1", EXPERTS), ("eps_clip", 1), ("eps_ln", 1), ("one", 1)):
    COLS[_name] = (sum(n for _, n in COLS.values()), _n)
NCOLS = sum(n for _, n in COLS.values())


def wait(eng, semaphore, count):
    if not isinstance(count, int) or count > 0:
        eng.wait_ge(semaphore, count)


def load_constants(nc, ctx, d):
    shapes = {
        "cols": [P, NCOLS], "ident": [P, P], "center": [P, P], "average": [P, P],
        "sel_d": [P, DG, P], "sum_n": [P, ND],
        "wz": [P, 2, DIN], "wbc": [P, 2, 2 * NSTATE], "wo": [P, 2, 2, P],
    }
    return {n: (ctx.enter_context(nc.sbuf_tensor("c_" + n, s, F32)), d[n]) for n, s in shapes.items()}


def token_phase(nc, c, h, w, d):
    with ExitStack() as ctx:
        def sb(name, shape, dt=F32):
            return ctx.enter_context(nc.sbuf_tensor(name, shape, dt))

        def sem(name):
            return ctx.enter_context(nc.semaphore(name))

        x = sb("x", [P, 2, 2, TOKENS + 2])
        tap = sb("tap", [P, TAPS, P])
        wx = sb("wx", [P, 2, DIN])
        conv_rep = sb("conv_rep", [P, 2, 2, DIN])
        xdt = sb("xdt", [RANK, 2, DIN])
        dtw = sb("dtw", [RANK, 2, DIN])
        stats = sb("stats", [P, PAIRS, 6])
        mv = sb("mv", [P, PAIRS, 2])
        dev = sb("dev", [P, PAIRS])
        dev2 = sb("dev2", [P, PAIRS])
        lnv = sb("lnv", [P, PAIRS])
        scale = sb("scale", [P, PAIRS])
        shift = sb("shift", [P, PAIRS])
        mean = sb("mean", [P, PAIRS])
        neg = sb("neg", [P, 2, TOKENS])
        ps_conv = ctx.enter_context(nc.psum_tensor("ps_conv", [P, 2, 512], F32))
        ps_stat = ctx.enter_context(nc.psum_tensor("ps_stat", [P, 2, 512], F32))
        ps_wdt = ctx.enter_context(nc.psum_tensor("ps_wdt", [P, 2, 512], F32))

        consts_in = sem("consts_in")
        weights_in = sem("weights_in")
        x_in = [sem("x_in0"), sem("x_in1")]
        x_free = sem("x_free")
        taps_made = sem("taps_made")
        slot_free = sem("slot_free")
        stat_done = sem("stat_done")
        agg_done = sem("agg_done")
        mean_ready = sem("mean_ready")
        dve = sem("dve")
        var_ready = sem("var_ready")
        rstd_steps = sem("rstd_steps")
        neg_made = sem("neg_made")
        h_done = sem("h_done")
        wdt_ready = sem("wdt_ready")
        act_weights = sem("act_weights")
        pool_weights = sem("pool_weights")
        loads = list(c.values())
        late = [(wx, d["wx"]), (conv_rep, d["conv_rep"]), (xdt, d["xdt"]), (dtw, d["dtw"])]

        def col(name, k=0, rows=P):
            at = COLS[name][0] + k
            return c["cols"][0][0:rows, at:at + 1]

        block = ctx.enter_context(nc.Block())

        @block.sync
        def _(sp):
            for name in ("cols", "ident"):
                t, src = c[name]
                sp.dma_start(t[:], src).then_inc(consts_in, 16)

            def load_x(pair, k):
                sp.wait_ge(x_free, pair + 1)
                sp.dma_start(x[:, k, :, 1:TOKENS + 1], d["x"][pair]).then_inc(x_in[k], 16)

            with sp.Fori(0, PAIRS // 2) as i:
                for k in range(2):
                    load_x(2 * i + k, k)

        @block.scalar
        def _(act):
            for name in ("center", "average"):
                t, src = c[name]
                act.dma_start(t[:], src).then_inc(consts_in, 16)
            for t, src in late:
                act.dma_start(t[:], src).then_inc(weights_in, 16)
            for name in ("wz", "wbc", "wo", "sel_d", "sum_n"):
                t, src = c[name]
                act.dma_start(t[:], src).then_inc(weights_in, 16)
            act.preload_act_table_set("natural_log_exp_and_others")
            act.sem_inc(slot_free, 2)
            act.wait_ge(consts_in, 64)
            with act.Fori(0, PAIRS // 2) as i:
                for k in range(2):
                    act.wait_ge(x_free, 2 * i + k + 3)
                    act.activation(h[:, 2 * i + k, :], ps_conv[:, k, 0:TOKENS], ACT.Identity,
                                   bias=col("tok_b")).then_inc(slot_free, 1)
            act.wait_ge(weights_in, 144)
            act.activation(w["decay"][:, 0, :], col2(c, "a_log"), ACT.Exp).then_inc(act_weights, 1)
            act.activation(c["wo"][0][:], c["wo"][0][:], ACT.Copy, scale=0.5).then_inc(act_weights, 1)
            act.wait_ge(wdt_ready, 1)
            act.activation(w["wdt"][:], ps_wdt[:, :, 0:DIN], ACT.Copy).then_inc(act_weights, 1)
            act.wait_ge(var_ready, 1)
            act.activation(lnv[:], ps_stat[:, 1, 0:PAIRS], ACT.Ln, bias=col("eps_clip")).then_inc(rstd_steps, 1)
            act.wait_ge(rstd_steps, 1)
            act.activation(scale[:], lnv[:], ACT.Exp, scale=-0.5).then_inc(rstd_steps, 1)
            act.wait_ge(act_weights, 3)

        @block.tensor
        def _(pe):
            pe.wait_ge(taps_made, TAPS)
            with pe.Fori(0, PAIRS // 2) as i:
                for k in range(2):
                    pe.wait_ge(x_in[k], 16 * i + 16)
                    pe.wait_ge(slot_free, 2 * i + k + 1)
                    for t, (parity, at) in enumerate(((1, 0), (0, 1), (1, 1), (0, 2), (1, 2))):
                        mm = pe.matmul(ps_conv[:, k, 0:TOKENS], tap[:, t, :], x[:, k, parity, at:at + TOKENS],
                                       start=(t == 0), stop=(t == TAPS - 1))
                    mm.then_inc(x_free, 1)
            pe.wait_ge(weights_in, 144)
            for r in range(2):
                mm = pe.matmul(ps_wdt[:, r, 0:DIN], xdt[:, r, :], dtw[:, r, :], start=True, stop=True)
            mm.then_inc(wdt_ready, 1)
            pe.wait_ge(consts_in, 64)
            pe.wait_ge(agg_done, PAIRS)
            pe.wait_ge(dve, 1)
            pe.matmul(ps_stat[:, 0, 0:PAIRS], c["average"][0][:], mean[:], start=True, stop=True).then_inc(mean_ready, 1)
            pe.wait_ge(dve, 4)
            pe.matmul(ps_stat[:, 1, 0:PAIRS], c["average"][0][:], dev2[:], start=True, stop=True).then_inc(var_ready, 1)

        @block.vector
        def _(v):
            v.memset(x[:, :, :, 0:TOKENS + 2:TOKENS + 1], 0.0).then_inc(x_free, 2)
            v.wait_ge(consts_in, 64)
            for t in range(TAPS):
                v.tensor_scalar(tap[:, t, :], c["ident"][0][:], col("tok_w", t), None, ALU.mult).then_inc(taps_made, 1)
            with v.Fori(0, PAIRS) as i:
                v.wait_ge(slot_free, i + 3)
                v.bn_stats(stats[:, i, :], h[:, i, :]).then_inc(stat_done, 1)
            v.wait_ge(stat_done, PAIRS)
            for n in range(PAIRS):
                v.bn_aggr(mv[:, n, :], stats[:, n, :]).then_inc(agg_done, 1)
            v.wait_ge(agg_done, PAIRS)
            v.tensor_copy(mean[:], mv[:, :, 0]).then_inc(dve, 1)
            v.wait_ge(mean_ready, 1)
            v.wait_ge(dve, 1)
            v.scalar_tensor_tensor(dev[:], ps_stat[:, 0, 0:PAIRS], -1.0, mean[:], ALU.mult, ALU.add).then_inc(dve, 1)
            v.wait_ge(dve, 2)
            v.tensor_tensor(dev2[:], dev[:], dev[:], ALU.mult).then_inc(dve, 1)
            v.wait_ge(dve, 3)
            v.tensor_tensor(dev2[:], dev2[:], mv[:, :, 1], ALU.add).then_inc(dve, 1)
            v.wait_ge(rstd_steps, 2)
            v.tensor_scalar(scale[:], scale[:], col("gamma"), None, ALU.mult).then_inc(dve, 1)
            v.wait_ge(dve, 5)
            v.scalar_tensor_tensor(shift[:], ps_stat[:, 0, 0:PAIRS], -1.0, scale[:], ALU.mult, ALU.mult).then_inc(dve, 1)
            v.wait_ge(dve, 6)
            v.tensor_scalar(shift[:], shift[:], col("beta"), None, ALU.add).then_inc(dve, 1)
            v.wait_ge(dve, 7)
            with v.Fori(0, PAIRS // 2) as i:
                for k in range(2):
                    n = 2 * i + k
                    tile = h[:, n, :]
                    v.tensor_scalar(tile, tile, scale[:, bass.ds(n, 1)], shift[:, bass.ds(n, 1)], ALU.mult,
                                    ALU.add).then_inc(neg_made, 1)
                    v.wait_ge(neg_made, 2 * n + 1)
                    v.tensor_scalar(neg[:, k, :], tile, 0.0, col("alpha"), ALU.min, ALU.mult).then_inc(neg_made, 1)
                    v.wait_ge(neg_made, 2 * n + 2)
                    v.scalar_tensor_tensor(tile, tile, 0.0, neg[:, k, :], ALU.max, ALU.add).then_inc(h_done, 1)
            v.wait_ge(h_done, PAIRS)

        @block.gpsimd
        def _(g):
            g.wait_ge(weights_in, 144)
            for r in range(2):
                src = wx[:, r, :].unsqueeze(1).to_broadcast([P, 2, DIN])
                g.tensor_tensor(w["wk"][:, r, :, :], src, conv_rep[:, r, :, :], ALU.mult).then_inc(pool_weights, 1)
            g.wait_ge(consts_in, 64)
            for r in range(2):
                g.tensor_scalar(w["skip"][:, r, :], c["ident"][0][:], col("D", r), None, ALU.mult).then_inc(pool_weights, 1)
            g.wait_ge(act_weights, 1)
            g.tensor_scalar(w["decay"][:, 1, :], w["decay"][:, 0, :], -1.0, None, ALU.mult).then_inc(pool_weights, 1)
            g.wait_ge(pool_weights, 5)


def col2(c, name):
    at, n = COLS[name]
    return c["cols"][0][:, at:at + n]


def stage_jobs(s, has_next, has_before):
    jobs = []
    if has_next:
        jobs += {0: ["cen"], 1: ["var"], 3: ["x0", "z0"], 4: ["x1", "z1"], 5: ["x2", "z2"], 6: ["x3", "z3"],
                 7: ["dt0", "dt1"], 8: ["dt2", "dt3"], 9: ["bc0"], 10: ["bc1"], 11: ["bc2"], 12: ["bc3"]}.get(s, [])
    if s == 2 and has_before:
        jobs.append("out1")
    if s == 11:
        jobs.append("out0")
    return jobs


def pair_jobs(has_next, has_before):
    return [j for s in range(STEPS) for j in stage_jobs(s, has_next, has_before)]


PROLOGUE = [j for j in pair_jobs(True, False) if j != "out0"]
N_PRO, N_FIRST, N_MID = len(PROLOGUE), len(pair_jobs(True, False)), len(pair_jobs(True, True))


class Jobs:

    def __init__(self, names, base, parity):
        self.names, self.base, self.parity = names, base, parity

    def number(self, job):
        return self.base + self.names.index(job)

    def bank(self, job):
        return (self.parity + self.names.index(job)) % 2


def jobs_of(pair, has_next, has_before):
    assert N_MID % 2 == 0
    if not has_before:
        return Jobs(pair_jobs(has_next, False), N_PRO, N_PRO % 2)
    return Jobs(pair_jobs(has_next, True), N_PRO + N_FIRST + N_MID * (pair - 1), (N_PRO + N_FIRST) % 2)


PROLOGUE_JOBS = Jobs(PROLOGUE, 0, 0)
_before_tail = N_PRO + N_FIRST + N_MID * (PAIRS - 2) + len(pair_jobs(False, True))
TAIL_JOBS = Jobs(["out1"], _before_tail, _before_tail % 2)


def mamba_phase(nc, c, h, w, bc_dram, dl_dram):
    with ExitStack() as ctx:
        def sb(name, shape, dt=F32):
            return ctx.enter_context(nc.sbuf_tensor(name, shape, dt))

        def ps(name, shape):
            return ctx.enter_context(nc.psum_tensor(name, shape, F32))

        def sem(name):
            return ctx.enter_context(nc.semaphore("m_" + name))

        T = TOKENS
        PAD = CTAPS - 1
        cen = sb("cen", [P, T])
        sq = sb("sq", [P, T])
        rstd = sb("rstd", [P, T])
        un = sb("un", [P, T + 2 * PAD])
        two = sb("two", [P, 2, T + 2 * PAD])
        xs = sb("xs", [P, 2, UNITS, T])
        sz = sb("sz", [P, 2, UNITS, T])
        dl = sb("dl", [P, UNITS, T])
        du = sb("du", [P, 2, UNITS, T])
        pre = sb("pre", [P, UNITS, T])
        tmp = sb("tmp", [P, UNITS, T])
        bc = sb("bc", [2 * NSTATE, UNITS, T])
        brep = sb("brep", [P, 2, NG, T])
        crep = sb("crep", [P, 2, NG, T])
        drep = sb("drep", [P, 2, DG, T])
        dec = sb("dec", [P, 4, NG * T + 1])
        st = sb("st", [P, 4, NG, T])
        yz = sb("yz", [P, 2, T])
        res = sb("res", [P, 2, T])
        ps_du = ps("ps_du", [P, 2, 512])
        ps_y = ps("ps_y", [P, 512])
        ps_job = ps("ps_job", [P, 2, 512])
        ps_b = ps("ps_b", [P, 3 * 512])

        zeroed = sem("zeroed")
        job_ready = sem("job_ready")
        job_taken = sem("job_taken")
        sq_ready = sem("sq_ready")
        rstd_ready = sem("rstd_ready")
        un_ready = sem("un_ready")
        two_in = sem("two_in")
        silu_ready = sem("silu_ready")
        softplus = sem("softplus")
        square_ready = sem("square_ready")
        delta_step = sem("delta_step")
        dl_ready = sem("dl_ready")
        dl_out = sem("dl_out")
        bc_out = sem("bc_out")
        du_ready = sem("du_ready")
        d_in = [sem("d_in0"), sem("d_in1")]
        b_in = [sem("b_in0"), sem("b_in1")]
        c_in = [sem("c_in0"), sem("c_in1")]
        du_rep = sem("du_rep")
        decay_ready = sem("decay_ready")
        drive_ready = sem("drive_ready")
        state_ready = sem("state_ready")
        weighted = sem("weighted")
        summed = sem("summed")
        gated = sem("gated")
        added = sem("added")

        def const(name):
            return c[name][0]

        def col(name, k=0):
            at = COLS[name][0] + k
            return c["cols"][0][:, at:at + 1]

        def decay_col(r, g, n):
            at = r * DG * NG + g * NG + n
            return w["decay"][:, 1, at:at + 1]

        def seg(r):
            return slice(1, T) if r == 0 else slice(0, T - 1)

        def arrivals(q, u):
            return 64 * (UNITS // 2 * q + u // 2 + 1)

        def run_pairs(prologue, pair_body, tail, engine):
            prologue()
            pair_body(0, 0, jobs_of(0, True, False), True, False)
            with engine.Fori(0, (PAIRS - 2) // 2) as i:
                for k in range(2):
                    q = 2 * i + 1 + k
                    pair_body(q, (1 + k) % 2, jobs_of(q, True, True), True, True)
            q = PAIRS - 1
            pair_body(q, q % 2, jobs_of(q, False, True), False, True)
            tail()

        block = ctx.enter_context(nc.Block())
        flat = "p a b -> p (a b)"

        @block.sync
        def _(sp):
            def stack(q):
                sp.wait_ge(un_ready, q + 1)
                for b in range(2):
                    rows = un[CH * b:CH * b + CH]
                    sp.dma_start(two[0:CH, b, :], rows).then_inc(two_in, 16)
                    sp.dma_start(two[CH:P, b, 0:T + 2 * PAD - 2], rows[:, 2:]).then_inc(two_in, 16)

            def write(q, k):
                sp.wait_ge(dl_ready, q + 1)
                sp.dma_start(dl_dram[k], dl[:]).then_inc(dl_out, 16)
                sp.wait_ge(job_taken, job_numbers(q).number("bc3") + 1)
                sp.dma_start(bc_dram[k], bc[:]).then_inc(bc_out, 16)

            numbers = {}

            def job_numbers(q):
                return numbers["of"]

            def read_delta(q, k, u):
                if u == 0:
                    sp.wait_ge(dl_out, 16 * (q + 1))
                wait(sp, decay_ready, DG * (UNITS * q + u - 1))
                for n in range(NN):
                    rows = slice(ND * n, ND * n + ND)
                    sp.dma_start(drep[rows, u % 2], dl_dram[k, :, u, :].rearrange("(g d) t -> d g t", g=DG))\
                      .then_inc(d_in[u % 2], 16)

            def read_states(q, k, u, first, buf, arrived, used):
                if u == 0:
                    sp.wait_ge(bc_out, 16 * (q + 1))
                wait(sp, used, DG * (UNITS * q + u - 1))
                for n in range(NN):
                    src = bc_dram[k, first + n:first + NSTATE:NN, u, :].unsqueeze(0).to_broadcast([ND, NG, T])
                    sp.dma_start(buf[ND * n:ND * n + ND, u % 2], src).then_inc(arrived[u % 2], 16)

            def read_b(q, k, u):
                read_states(q, k, u, 0, brep, b_in, drive_ready)

            def read_c(q, k, u):
                read_states(q, k, u, NSTATE, crep, c_in, weighted)

            def prologue():
                numbers["of"] = PROLOGUE_JOBS
                stack(0)
                write(0, 0)
                for read in (read_delta, read_b, read_c):
                    read(0, 0, 0)

            def pair_body(q, k, jobs, has_next, has_before):
                numbers["of"] = jobs
                read_delta(q, k, 1)
                read_b(q, k, 1)
                if has_next:
                    stack(q + 1)
                read_c(q, k, 1)
                for u in (2, 3):
                    for read in (read_delta, read_b, read_c):
                        read(q, k, u)
                if has_next:
                    write(q + 1, 1 - k)
                    for read in (read_delta, read_b, read_c):
                        read(q + 1, 1 - k, 0)

            run_pairs(prologue, pair_body, lambda: None, sp)

        @block.tensor
        def _(pe):
            def project(jobs, name, q, kq):
                kind, u = name[:-1], ord(name[-1]) - ord("0")
                b, r = u // 2, u % 2
                if name == "var":
                    pe.wait_ge(sq_ready, q + 1)
                elif kind in ("x", "z"):
                    pe.wait_ge(two_in, 64 * (q + 1))
                elif kind in ("dt", "bc"):
                    pe.wait_ge(silu_ready, 2 * q + 1)
                elif kind == "out":
                    b = u
                    pe.wait_ge(gated, UNITS * q + 2 * b + 2)
                wait(pe, job_taken, jobs.number(name) - 1)
                out = ps_job[:, jobs.bank(name), 0:T]
                if name == "cen":
                    products = [(const("center")[:], h[:, q, :])]
                elif name == "var":
                    products = [(const("average")[:], sq[:])]
                elif kind == "x":
                    starts = (0, 1) if r == 0 else (PAD + 1, PAD)
                    products = [(w["wk"][:, r, i, :], two[:, b, at:at + T]) for i, at in enumerate(starts)]
                elif kind == "z":
                    products = [(const("wz")[:, r, :], two[:, b, PAD:PAD + T])]
                elif kind == "dt":
                    products = [(w["wdt"][:, r, :], xs[:, kq, u, :])]
                elif kind == "bc":
                    out = out[0:2 * NSTATE]
                    products = [(const("wbc")[:, r, :], xs[:, kq, u, :])]
                else:
                    products = [(const("wo")[:, r, b, :], yz[:, r, :]) for r in range(2)]
                for i, (weight, moving) in enumerate(products):
                    mm = pe.matmul(out, weight, moving, start=(i == 0), stop=(i == len(products) - 1))
                mm.then_inc(job_ready, 1)

            def replicate_du(step, q, k, s):
                u, g = divmod(s, DG)
                pe.wait_ge(du_ready, q + 1)
                wait(pe, drive_ready, step - 1)
                pe.matmul(ps_du[:, s % 2, 0:T], const("sel_d")[:, g, :], du[:, k, u, :], start=True,
                          stop=True).then_inc(du_rep, 1)

            def sum_states(step, unit, k, s):
                u, g = divmod(s, DG)
                if g == 1:
                    wait(pe, gated, unit)
                    pe.matmul(ps_y[:, 0:T], w["skip"][:, u % 2, :], xs[:, k, u, :], start=True, stop=False,
                              skip_group_check=True)
                pe.wait_ge(weighted, step + 1)
                for n in range(NG):
                    for back in (1, 0):
                        rows = slice(ND * (g - back), ND * (g - back) + ND)
                        mm = pe.matmul(ps_y[rows, 0:T], const("sum_n")[:], st[:, (s - back) % 4, n, :], start=False,
                                       stop=(n == NG - 1), skip_group_check=True)
                mm.then_inc(summed, 2)

            def prologue():
                pe.wait_ge(zeroed, 1)
                for name in PROLOGUE:
                    project(PROLOGUE_JOBS, name, 0, 0)
                replicate_du(0, 0, 0, 0)

            def pair_body(q, k, jobs, has_next, has_before):
                for s in range(STEPS):
                    step = STEPS * q + s
                    if s + 1 < STEPS:
                        replicate_du(step + 1, q, k, s + 1)
                    elif has_next:
                        replicate_du(step + 1, q + 1, 1 - k, 0)
                    for name in stage_jobs(s, has_next, has_before):
                        if name == "out1":
                            project(jobs, name, q - 1, None)
                        elif name == "out0":
                            project(jobs, name, q, None)
                        else:
                            project(jobs, name, q + 1, 1 - k)
                    if s > 1 and s % 2 == 1:
                        sum_states(step - 2, UNITS * q + (s - 2) // DG, k, s - 2)
                    elif s == 1 and has_before:
                        sum_states(step - 2, UNITS * q - 1, 1 - k, STEPS - 1)

            def tail():
                q = PAIRS - 1
                sum_states(STEPS * q + STEPS - 1, UNITS * q + UNITS - 1, q % 2, STEPS - 1)
                project(TAIL_JOBS, "out1", q, None)

            run_pairs(prologue, pair_body, tail, pe)

        @block.scalar
        def _(act):
            def take(jobs, name, out, func=ACT.Copy, bias=None):
                act.wait_ge(job_ready, jobs.number(name) + 1)
                bank = ps_job[0:out.shape[0], jobs.bank(name), 0:T]
                if bias is None:
                    act.activation(out, bank, func).then_inc(job_taken, 1)
                else:
                    act.activation(out, bank, func, bias=bias).then_inc(job_taken, 1)

            def do_job(jobs, name, q, k):
                kind, u = name[:-1], ord(name[-1]) - ord("0")
                if name == "cen":
                    take(jobs, name, cen[:])
                    act.wait_ge(job_taken, jobs.number(name) + 1)
                    act.activation(sq[:], cen[:], ACT.Square).then_inc(sq_ready, 1)
                elif name == "var":
                    take(jobs, name, sq[:], ACT.Ln, col("eps_ln"))
                    act.wait_ge(job_taken, jobs.number(name) + 1)
                    act.activation(rstd[:], sq[:], ACT.Exp, scale=-0.5).then_inc(rstd_ready, 1)
                elif kind == "x":
                    take(jobs, name, xs[:, k, u, :], ACT.Identity, col("conv_b", u % 2))
                elif kind == "z":
                    if u == 0:
                        wait(act, gated, UNITS * (q - 1))
                    take(jobs, name, sz[:, k, u, :])
                elif kind == "dt":
                    take(jobs, name, pre[:, u, :], ACT.Identity, col("dt_b", u % 2))
                elif kind == "bc":
                    if u == 0:
                        wait(act, bc_out, 16 * q)
                    take(jobs, name, bc[:, u, :])
                elif kind == "out":
                    wait(act, added, 2 * q + u - 1)
                    take(jobs, name, res[:, u, :])

            def silus(jobs, k):
                act.preload_act_table_set("silu_and_others")
                act.wait_ge(job_taken, jobs.number("z3") + 1)
                for t in (xs, sz):
                    act.activation(t[:, k], t[:, k], ACT.Silu).then_inc(silu_ready, 1)
                act.preload_act_table_set("natural_log_exp_and_others")

            def softplus_steps(jobs, q, k):
                act.wait_ge(job_taken, jobs.number("dt3") + 1)
                act.activation(tmp[:], pre[:], ACT.Abs).then_inc(softplus, 1)
                act.wait_ge(softplus, 3 * q + 1)
                act.activation(tmp[:], tmp[:], ACT.Exp, scale=-1.0).then_inc(softplus, 1)
                act.wait_ge(softplus, 3 * q + 2)
                act.activation(du[:, k], tmp[:], ACT.Square).then_inc(square_ready, 1)
                wait(act, dl_out, 16 * q)
                act.activation(dl[:], tmp[:], ACT.Ln, bias=col("one")).then_inc(softplus, 1)

            def decays(step, q, s):
                u, g = divmod(s, DG)
                r = u % 2
                act.wait_ge(d_in[u % 2], arrivals(q, u))
                wait(act, state_ready, step - 3)
                for n in range(NG):
                    ins = act.activation(dec[:, s % 4, n * T + 1:n * T + T], drep[:, u % 2, g, seg(r)], ACT.Exp,
                                         scale=decay_col(r, g, n))
                ins.then_inc(decay_ready, 1)

            def prologue():
                act.preload_act_table_set("natural_log_exp_and_others")
                for name in PROLOGUE:
                    do_job(PROLOGUE_JOBS, name, 0, 0)
                    if name == "z3":
                        silus(PROLOGUE_JOBS, 0)
                    if name == "dt3":
                        softplus_steps(PROLOGUE_JOBS, 0, 0)
                act.wait_ge(zeroed, 1)
                for s in range(AHEAD):
                    decays(s, 0, s)

            def pair_body(q, k, jobs, has_next, has_before):
                for s in range(STEPS):
                    step = STEPS * q + s
                    if s + AHEAD < STEPS:
                        decays(step + AHEAD, q, s + AHEAD)
                    elif has_next:
                        decays(step + AHEAD, q + 1, s + AHEAD - STEPS)
                    for name in stage_jobs(s, has_next, has_before):
                        if name == "out1":
                            do_job(jobs, name, q - 1, None)
                        elif name == "out0":
                            do_job(jobs, name, q, None)
                        else:
                            do_job(jobs, name, q + 1, 1 - k)
                    if has_next and s == 6:
                        silus(jobs, 1 - k)
                    if has_next and s == 8:
                        softplus_steps(jobs, q + 1, 1 - k)

            def tail():
                do_job(TAIL_JOBS, "out1", PAIRS - 1, None)

            run_pairs(prologue, pair_body, tail, act)

        @block.vector
        def _(v):
            def normalize(q):
                v.wait_ge(rstd_ready, q + 1)
                wait(v, two_in, 64 * q)
                v.tensor_tensor(un[:, PAD:PAD + T], cen[:], rstd[:], ALU.mult).then_inc(un_ready, 1)

            def delta(q, k):
                d_, p_ = dl[:].rearrange(flat), tmp[:].rearrange(flat)
                v.wait_ge(softplus, 3 * q + 3)
                v.wait_ge(square_ready, q + 1)
                v.scalar_tensor_tensor(p_, du[:, k].rearrange(flat), -0.5, p_, ALU.mult, ALU.add).then_inc(delta_step, 1)
                v.wait_ge(delta_step, 2 * q + 1)
                v.scalar_tensor_tensor(d_, d_, -LOG_MARGIN, p_, ALU.add, ALU.max).then_inc(delta_step, 1)
                v.wait_ge(delta_step, 2 * q + 2)
                v.scalar_tensor_tensor(d_, pre[:].rearrange(flat), 0.0, d_, ALU.max, ALU.add).then_inc(dl_ready, 1)

            def scan(step, q, s):
                u, g = divmod(s, DG)
                r = u % 2
                v.wait_ge(du_rep, step + 1)
                if g == 0:
                    v.wait_ge(b_in[u % 2], arrivals(q, u))
                wait(v, state_ready, step)
                drive = ps_b[:, 0:NG * T]
                v.tensor_tensor(drive.rearrange("p (a b) -> p a b", a=NG),
                                ps_du[:, s % 2, 0:T].unsqueeze(1).to_broadcast([P, NG, T]),
                                brep[:, u % 2], ALU.mult).then_inc(drive_ready, 1)
                v.wait_ge(drive_ready, step + 1)
                v.wait_ge(decay_ready, step + 1)
                wait(v, summed, step - 3)
                order = slice(None) if r == 0 else slice(None, None, -1)
                v.tensor_tensor_scan(st[:, s % 4].rearrange(flat)[:, order], dec[:, s % 4, r:r + NG * T][:, order],
                                     drive[:, order], 0.0, ALU.mult, ALU.add).then_inc(state_ready, 1)

            def gate(unit, k, u, last_read):
                v.wait_ge(summed, DG * unit + DG)
                if last_read is not None:
                    v.wait_ge(job_ready, last_read)
                v.tensor_tensor(yz[:, u % 2, :], ps_y[:, 0:T], sz[:, k, u, :], ALU.mult).then_inc(gated, 1)

            def prologue():
                v.memset(dec[:, :, 0:NG * T + 1:T], 0.0)
                v.memset(un[:, 0:PAD], 0.0)
                v.memset(un[:, PAD + T:], 0.0).then_inc(zeroed, 1)
                v.wait_ge(zeroed, 1)
                normalize(0)
                delta(0, 0)

            def pair_body(q, k, jobs, has_next, has_before):
                for s in range(STEPS):
                    step = STEPS * q + s
                    u = s // DG
                    scan(step, q, s)
                    if s % DG == 1:
                        if u > 0:
                            read = {1: "out1" if has_before else None, 3: "out0"}.get(u)
                            gate(UNITS * q + u - 1, k, u - 1, None if read is None else jobs.number(read) + 1)
                        elif has_before:
                            gate(UNITS * q - 1, 1 - k, UNITS - 1, None)
                    if has_next and s == 1:
                        normalize(q + 1)
                    if has_next and s == 11:
                        delta(q + 1, 1 - k)

            def tail():
                q = PAIRS - 1
                gate(UNITS * q + UNITS - 1, q % 2, UNITS - 1, None)

            run_pairs(prologue, pair_body, tail, v)

        @block.gpsimd
        def _(g):
            def drive_input(q, k):
                g.wait_ge(dl_ready, q + 1)
                g.wait_ge(silu_ready, 2 * q + 1)
                g.tensor_tensor(du[:, k], dl[:], xs[:, k], ALU.mult).then_inc(du_ready, 1)

            def weight_states(step, q, s):
                u = s // DG
                g.wait_ge(c_in[u % 2], arrivals(q, u))
                g.wait_ge(state_ready, step + 1)
                g.tensor_tensor(st[:, s % 4], st[:, s % 4], crep[:, u % 2], ALU.mult).then_inc(weighted, 1)

            def add(q, b):
                g.tensor_tensor(h[:, q, :], h[:, q, :], res[:, b, :], ALU.add).then_inc(added, 1)

            def prologue():
                drive_input(0, 0)

            def pair_body(q, k, jobs, has_next, has_before):
                for s in range(STEPS):
                    b = {3: 1 if has_before else None, 12: 0}.get(s)
                    if b is not None:
                        g.wait_ge(job_taken, jobs.number(f"out{b}") + 1)
                    weight_states(STEPS * q + s, q, s)
                    if b is not None:
                        add(q - b, b)
                    if has_next and s == 11:
                        drive_input(q + 1, 1 - k)

            def tail():
                g.wait_ge(job_taken, TAIL_JOBS.base + 1)
                add(PAIRS - 1, 1)
                g.wait_ge(added, 2 * PAIRS)

            run_pairs(prologue, pair_body, tail, g)


def expert_phase(nc, c, h, d, out):
    with ExitStack() as ctx:
        def sb(name, shape):
            return ctx.enter_context(nc.sbuf_tensor(name, shape, F32))

        def ps(name, shape):
            return ctx.enter_context(nc.psum_tensor(name, shape, F32))

        def sem(name):
            return ctx.enter_context(nc.semaphore("e_" + name))

        T, E, R = TOKENS, EXPERTS, 2 * CHUNKS
        w1 = sb("w1", [P, 2, E, HID])
        w2 = sb("w2", [HID, E, CH])
        b2 = sb("b2", [R * E, R * CH])
        gate_w = sb("gate_w", [P, 2, E])
        gate_b = sb("gate_b", [P, R, E])
        rank = sb("rank", [P, R, E])
        cen = sb("cen2", [P, T])
        sq = sb("sq2", [P, T])
        rstd = sb("rstd2", [P, T])
        un = sb("un2", [P, 2, T])
        hc = sb("hc", [P, T])
        act_h = sb("act_h", [P, 2, E, T])
        lg = sb("lg", [CT, R, E])
        pr = sb("pr", [CT, R, E])
        hit = sb("hit", [CT, R, E])
        one1 = sb("one1", [CT, R, E])
        one2 = sb("one2", [CT, R, E])
        mx = sb("mx", [CT, R])
        cw = sb("cw", [CT, 2, R, E])
        cwt = sb("cwt", [R * E, CT])
        prod = sb("prod", [CT, 2, E, CH])
        red = sb("red", [CT, 2, R, CH])
        tok = sb("tok", [CT, 2, R, CH])
        ps_h = ps("ps_h", [P, 2, 512])
        ps_e = ps("ps_e", [P, 2, 512])
        ps_t = ps("ps_t", [P, 512])
        ps_n = ps("ps_n", [P, 512])
        ps_g = ps("ps_g", [P, 512])

        loaded = sem("loaded")
        cen_ready = sem("cen_ready")
        cen_taken = sem("cen_taken")
        sq_ready = sem("sq_ready")
        var_ready = sem("var_ready")
        var_taken = sem("var_taken")
        rstd_ready = sem("rstd_ready")
        un_ready = sem("un_ready")
        logits_ready = sem("logits_ready")
        shifted = sem("shifted")
        exps_ready = sem("exps_ready")
        dve = sem("dve")
        cw_ready = sem("cw_ready")
        cwt_ready = sem("cwt_ready")
        cwt_taken = sem("cwt_taken")
        hc_ready = sem("hc_ready")
        base_ready = sem("base_ready")
        base_taken = sem("base_taken")
        hid_ready = sem("hid_ready")
        hid_taken = sem("hid_taken")
        out_ready = sem("out_ready")
        out_taken = sem("out_taken")
        reduced = sem("reduced")
        finished = sem("finished")
        stored = [sem("stored0"), sem("stored1")]

        def const(name):
            return c[name][0]

        def col(name, k=0):
            at = COLS[name][0] + k
            return c["cols"][0][:, at:at + 1]

        GATE_STEPS = 17
        AFTER = {2: 0, 5: 1, 7: 2}

        def run_pairs(prologue, pair_body, tail, engine):
            prologue()
            pair_body(0, 0, True, False, 0)
            with engine.Fori(0, (PAIRS - 2) // 2) as i:
                for k in range(2):
                    pair_body(2 * i + 1 + k, (1 + k) % 2, True, True, i + 1)
            pair_body(PAIRS - 1, (PAIRS - 1) % 2, False, True, PAIRS // 2)
            tail()

        block = ctx.enter_context(nc.Block())
        loads = [(w1, "w1"), (w2, "w2"), (b2, "b2"), (gate_w, "gate_w"), (gate_b, "gate_b"), (rank, "rank")]

        @block.sync
        def _(sp):
            for t, name in loads:
                sp.dma_start(t[:], d[name]).then_inc(loaded, 16)

            def prologue():
                pass

            def pair_body(q, k, has_next, has_before, turn):
                if has_before:
                    store(q - 1, 1 - k)

            def store(q, k):
                sp.wait_ge(finished, q + 1)
                for b in range(2):
                    sp.dma_start(out[2 * q + b].rearrange("(p c) n -> p c n", c=CHUNKS),
                                 tok[:, k, CHUNKS * b:CHUNKS * b + CHUNKS, :]).then_inc(stored[k], 16)

            run_pairs(prologue, pair_body, lambda: store(PAIRS - 1, (PAIRS - 1) % 2), sp)
            for k in range(2):
                sp.wait_ge(stored[k], 16 * 2 * (PAIRS // 2))

        @block.tensor
        def _(pe):
            def center(q):
                wait(pe, cen_taken, q)
                pe.matmul(ps_n[:, 0:T], const("center")[:], h[:, q, :], start=True, stop=True).then_inc(cen_ready, 1)

            def variance(q):
                pe.wait_ge(sq_ready, q + 1)
                pe.wait_ge(cen_taken, q + 1)
                pe.matmul(ps_n[:, 0:T], const("average")[:], sq[:], start=True, stop=True).then_inc(var_ready, 1)

            def logits(q, k):
                pe.wait_ge(un_ready, q + 1)
                wait(pe, cwt_taken, q)
                for b in range(2):
                    for ch in range(CHUNKS):
                        at = (b * CHUNKS + ch) * E
                        mm = pe.matmul(ps_g[0:CT, at:at + E], un[:, k, ch:T:CHUNKS], gate_w[:, b, :], start=True, stop=True)
                mm.then_inc(logits_ready, 1)

            def turn_weights(q, k):
                pe.wait_ge(cw_ready, q + 1)
                pe.matmul(ps_g[0:R * E, 0:CT], cw[:, k].rearrange("p a b -> p (a b)"), const("ident")[0:CT, 0:CT],
                          start=True, stop=True).then_inc(cwt_ready, 1)

            def base(q):
                pe.wait_ge(cwt_taken, q + 1)
                pe.wait_ge(hc_ready, q + 1)
                wait(pe, base_taken, q)
                pe.matmul(ps_t[0:CT, 0:R * CH], cwt[:], b2[:], start=True, stop=False, skip_group_check=True)
                rows = ps_t[0:CT, 0:R * CH].rearrange("p (b c n) -> p b c n", b=2, c=CHUNKS)
                for ch in range(CHUNKS):
                    mm = pe.matmul(rows[:, :, ch, :], hc[:, ch:T:CHUNKS], const("ident")[:], start=False,
                                   stop=(ch == CHUNKS - 1), skip_group_check=True)
                mm.then_inc(base_ready, 1)

            def hidden(q, k, b, e):
                n = (2 * q + b) * E + e
                wait(pe, hid_taken, n - 1)
                pe.matmul(ps_h[:, e % 2, 0:T], w1[:, b, e, :], un[:, k, :], start=True, stop=True).then_inc(hid_ready, 1)

            def experts_out(q, b, ch):
                n = (2 * q + b) * CHUNKS + ch
                pe.wait_ge(hid_taken, (2 * q + b) * E + E)
                wait(pe, out_taken, n - 1)
                for e in range(E):
                    mm = pe.matmul(ps_e[0:CT, (b * CHUNKS + ch) % 2, e * CH:e * CH + CH], act_h[:, b, e, ch:T:CHUNKS],
                                   w2[:, e, :], start=True, stop=True)
                mm.then_inc(out_ready, 1)

            def prologue():
                pe.wait_ge(loaded, 16 * len(loads))
                center(0)
                variance(0)
                logits(0, 0)
                turn_weights(0, 0)
                base(0)

            def pair_body(q, k, has_next, has_before, turn):
                for b in range(2):
                    for e in range(E):
                        hidden(q, k, b, e)
                        if e in AFTER and (b or has_before):
                            experts_out(q if b else q - 1, 1 - b, AFTER[e])
                        if has_next:
                            if (b, e) == (0, 0):
                                center(q + 1)
                            if (b, e) == (0, 2):
                                variance(q + 1)
                            if (b, e) == (0, 6):
                                logits(q + 1, 1 - k)
                            if (b, e) == (1, 5):
                                turn_weights(q + 1, 1 - k)
                            if (b, e) == (1, 7):
                                base(q + 1)

            def tail():
                for ch in range(CHUNKS):
                    experts_out(PAIRS - 1, 1, ch)

            run_pairs(prologue, pair_body, tail, pe)

        @block.scalar
        def _(act):
            def squares(q):
                act.wait_ge(cen_ready, q + 1)
                wait(act, un_ready, q)
                act.activation(cen[:], ps_n[:, 0:T], ACT.Copy).then_inc(cen_taken, 1)
                act.wait_ge(cen_taken, q + 1)
                wait(act, rstd_ready, q)
                act.activation(sq[:], cen[:], ACT.Square).then_inc(sq_ready, 1)

            def inverse_deviation(q):
                act.wait_ge(var_ready, q + 1)
                act.activation(sq[:], ps_n[:, 0:T], ACT.Ln, bias=col("eps_ln")).then_inc(var_taken, 1)
                act.wait_ge(var_taken, q + 1)
                act.activation(rstd[:], sq[:], ACT.Exp, scale=-0.5).then_inc(rstd_ready, 1)

            def exps(q):
                act.wait_ge(shifted, q + 1)
                act.activation(pr[:], lg[:], ACT.Exp).then_inc(exps_ready, 1)

            def take_cwt(q):
                act.wait_ge(cwt_ready, q + 1)
                wait(act, base_ready, q)
                act.activation(cwt[:], ps_g[0:R * E, 0:CT], ACT.Copy).then_inc(cwt_taken, 1)

            def take_base(q, k):
                act.wait_ge(base_ready, q + 1)
                act.activation(tok[:, k].rearrange("p a b -> p (a b)"), ps_t[0:CT, 0:R * CH], ACT.Copy)\
                   .then_inc(base_taken, 1)

            def gelu(q, b, e):
                n = (2 * q + b) * E + e
                act.wait_ge(hid_ready, n + 1)
                if e == 0:
                    wait(act, out_ready, (2 * q + b - 1) * CHUNKS)
                act.activation(act_h[:, b, e, :], ps_h[:, e % 2, 0:T], ACT.Gelu, bias=col("b1", e)).then_inc(hid_taken, 1)

            def natural():
                act.preload_act_table_set("natural_log_exp_and_others")

            def prologue():
                natural()
                squares(0)
                inverse_deviation(0)
                exps(0)
                take_cwt(0)
                take_base(0, 0)
                act.preload_act_table_set("gelu_and_others")

            def pair_body(q, k, has_next, has_before, turn):
                for b in range(2):
                    for e in range(E):
                        gelu(q, b, e)
                        if has_next:
                            if (b, e) == (0, 0):
                                squares(q + 1)
                            if (b, e) == (0, 2):
                                natural()
                                inverse_deviation(q + 1)
                                act.preload_act_table_set("gelu_and_others")
                            if (b, e) == (1, 0):
                                natural()
                                exps(q + 1)
                                act.preload_act_table_set("gelu_and_others")
                            if (b, e) == (1, 5):
                                take_cwt(q + 1)
                            if (b, e) == (1, 7):
                                if has_before:
                                    act.wait_ge(stored[1 - k], 2 * 16 * turn)
                                take_base(q + 1, 1 - k)

            run_pairs(prologue, pair_body, lambda: None, act)

        @block.vector
        def _(v):
            def normalize(q, k):
                v.wait_ge(rstd_ready, q + 1)
                wait(v, hid_ready, 2 * E * (q - 1))
                v.tensor_tensor(un[:, k, :], cen[:], rstd[:], ALU.mult).then_inc(un_ready, 1)

            def wide(t):
                return t[:].unsqueeze(2).to_broadcast([CT, R, E])

            class Chain:

                def __init__(self, q):
                    self.count = GATE_STEPS * q

                def then(self, ins):
                    ins.then_inc(dve, 1)
                    self.count = self.count + 1
                    v.wait_ge(dve, self.count)

            def shift_logits(q):
                v.wait_ge(logits_ready, q + 1)
                wait(v, exps_ready, q)
                ch = Chain(q)
                ch.then(v.tensor_tensor(lg[:], ps_g[0:CT, 0:R * E].rearrange("p (a b) -> p a b", a=R), gate_b[0:CT],
                                        ALU.add))
                ch.then(v.tensor_reduce(mx[:], lg[:], AX.X, ALU.max))
                v.tensor_tensor(lg[:], lg[:], wide(mx), ALU.subtract).then_inc(shifted, 1)
                return ch

            def choose(q, k, ch):
                v.wait_ge(exps_ready, q + 1)
                ch.then(v.tensor_reduce(mx[:], pr[:], AX.X, ALU.add))
                ch.then(v.reciprocal(mx[:], mx[:]))
                ch.then(v.tensor_tensor(pr[:], pr[:], wide(mx), ALU.mult))
                ch.then(v.tensor_reduce(mx[:], pr[:], AX.X, ALU.max))
                ch.then(v.tensor_tensor(hit[:], pr[:], wide(mx), ALU.is_equal))
                ch.then(v.tensor_tensor(hit[:], hit[:], rank[0:CT], ALU.mult))
                ch.then(v.tensor_reduce(mx[:], hit[:], AX.X, ALU.max))
                ch.then(v.tensor_tensor(one1[:], hit[:], wide(mx), ALU.is_equal))
                ch.then(v.scalar_tensor_tensor(one2[:], one1[:], -2.0, pr[:], ALU.mult, ALU.add))
                ch.then(v.tensor_reduce(mx[:], one2[:], AX.X, ALU.max))
                ch.then(v.tensor_tensor(hit[:], one2[:], wide(mx), ALU.is_equal))
                ch.then(v.tensor_tensor(hit[:], hit[:], rank[0:CT], ALU.mult))
                ch.then(v.tensor_reduce(mx[:], hit[:], AX.X, ALU.max))
                ch.then(v.tensor_tensor(one2[:], hit[:], wide(mx), ALU.is_equal))
                ch.then(v.tensor_tensor(one1[:], one1[:], one2[:], ALU.add))
                v.tensor_tensor(cw[:, k], pr[:], one1[:], ALU.mult).then_inc(cw_ready, 1)

            def take_chunk(q, k, b, ch):
                n = (2 * q + b) * CHUNKS + ch
                row = b * CHUNKS + ch
                v.wait_ge(out_ready, n + 1)
                v.tensor_tensor(prod[:, row % 2], ps_e[0:CT, row % 2, :].rearrange("p (e n) -> p e n", e=E),
                                cw[:, k, row, :].unsqueeze(2).to_broadcast([CT, E, CH]), ALU.mult).then_inc(out_taken, 1)
                v.wait_ge(out_taken, n + 1)
                v.tensor_reduce(red[:, k, row, :], prod[:, row % 2].rearrange("p e n -> p n e"), AX.X, ALU.add)\
                 .then_inc(reduced, 1)

            def finish(q, k):
                v.wait_ge(reduced, R * (q + 1))
                v.wait_ge(base_taken, q + 1)
                v.tensor_tensor(tok[:, k], tok[:, k], red[:, k], ALU.add).then_inc(finished, 1)

            def prologue():
                v.wait_ge(loaded, 16 * len(loads))
                normalize(0, 0)
                choose(0, 0, shift_logits(0))

            def pair_body(q, k, has_next, has_before, turn):
                chain = None
                for b in range(2):
                    for e in range(E):
                        if e in AFTER and (b or has_before):
                            take_chunk(q if b else q - 1, k if b else 1 - k, 1 - b, AFTER[e])
                        if has_before and (b, e) == (0, 7):
                            finish(q - 1, 1 - k)
                        if has_next:
                            if (b, e) == (0, 3):
                                normalize(q + 1, 1 - k)
                            if (b, e) == (1, 0):
                                chain = shift_logits(q + 1)
                            if (b, e) == (1, 3):
                                choose(q + 1, 1 - k, chain)

            def tail():
                for ch in range(CHUNKS):
                    take_chunk(PAIRS - 1, (PAIRS - 1) % 2, 1, ch)
                finish(PAIRS - 1, (PAIRS - 1) % 2)

            run_pairs(prologue, pair_body, tail, v)

        @block.gpsimd
        def _(g):
            def copy_h(q):
                wait(g, base_ready, q)
                g.tensor_copy(hc[:], h[:, q, :]).then_inc(hc_ready, 1)

            run_pairs(lambda: copy_h(0), lambda q, k, n, b, t: copy_h(q + 1) if n else None, lambda: None, g)


def build(nc, d, out, scratch):
    with ExitStack() as ctx:
        c = load_constants(nc, ctx, d)
        h = ctx.enter_context(nc.sbuf_tensor("h", [P, PAIRS, TOKENS], F32))
        with ExitStack() as own:
            w = {n: own.enter_context(nc.sbuf_tensor("w_" + n, s, dt)) for n, s, dt in (
                ("decay", [P, 2, 2 * DG * NG], F32), ("wk", [P, 2, 2, DIN], F32), ("skip", [P, 2, P], F32),
                ("wdt", [P, 2, DIN], F32))}
            token_phase(nc, c, h, w, d)
            mamba_phase(nc, c, h, w, scratch[0], scratch[1])
        expert_phase(nc, c, h, d, out)


def layouts(np, i):
    f = np.float32
    both = lambda a: np.concatenate([a, a], axis=0)
    arrays = {"x": i["x"].reshape(PAIRS, 2, TOKENS, 2, CH).transpose(0, 1, 4, 3, 2).reshape(PAIRS, P, 2, TOKENS)}
    cols = np.zeros((P, NCOLS), f)

    def put(name, value, k=0):
        value = np.asarray(value)
        value = value.reshape(P, -1)
        at = COLS[name][0] + k
        cols[:, at:at + value.shape[1]] = value

    put("tok_w", both(i["L0_tok_w"].reshape(TAPS, CH).T))
    for name, key in (("tok_b", "L0_tok_b"), ("gamma", "L0_tok_gamma"), ("beta", "L0_tok_beta"), ("alpha", "L0_tok_alpha")):
        put(name, both(i[key]))
    put("b1", i["L0_ffn_b1"].T)
    put("eps_clip", np.full(P, 1e-3, f))
    put("eps_ln", np.full(P, 1e-5, f))
    put("one", np.ones(P, f))
    wx, wz = np.zeros((P, 2, DIN), f), np.zeros((P, 2, DIN), f)
    wo = np.zeros((DIN, 2, 2, P), f)
    wbc, conv_rep = np.zeros((DIN, 2, 2 * NSTATE), f), np.zeros((P, 2, 2, DIN), f)
    xdt, dtw = np.zeros((RANK, 2, DIN), f), np.zeros((RANK, 2, DIN), f)
    for r, n in enumerate("fb"):
        g = lambda name: i[f"L0_attn_{n}_{name}"]
        put("conv_b", g("conv_b"), r)
        put("dt_b", g("dt_b"), r)
        put("D", g("D"), r)
        a = g("A_log").reshape(DG, ND, NG, NN).transpose(3, 1, 0, 2).reshape(P, DG * NG)
        put("a_log", a, r * DG * NG)
        for b in range(2):
            rows = slice(CH * b, CH * b + CH)
            wx[rows, r] = g("in_w")[0:DIN].T
            for two in range(2):
                conv_rep[rows, r, two] = g("conv_w")[:, (2 * b if r == 0 else 2 - 2 * b) + two]
            wo[:, r, b, rows] = g("out_w").T
        wz[0:CH, r] = g("in_w")[DIN:2 * DIN].T
        wbc[:, r] = g("xproj_w")[RANK:].T
        xdt[:, r] = g("xproj_w")[0:RANK]
        dtw[:, r] = g("dt_w").T
    w1, gate_w = np.zeros((P, 2, EXPERTS, HID), f), np.zeros((P, 2, EXPERTS), f)
    rows_of = 2 * CHUNKS
    b2 = np.zeros((rows_of, EXPERTS, rows_of, CH), f)
    for b in range(2):
        rows = slice(CH * b, CH * b + CH)
        w1[rows, b] = i["L0_ffn_W1"].transpose(1, 0, 2)
        gate_w[rows, b] = i["L0_ffn_gate_w"]
    for n in range(rows_of):
        b2[n, :, n] = i["L0_ffn_b2"]
    channel = np.arange(P) // CH
    same = (channel[:, None] == channel[None, :]).astype(f) / f(CH)
    row = np.arange(P)
    d_of, n_of = row % ND, row // ND
    sel_d = np.zeros((P, DG, P), f)
    for g_ in range(DG):
        sel_d[ND * g_ + d_of, g_, row] = 1
    sum_n = np.zeros((P, ND), f)
    sum_n[row, d_of] = 1
    arrays.update(
        cols=cols, ident=np.eye(P, dtype=f), center=np.eye(P, dtype=f) - same, average=same, sel_d=sel_d, sum_n=sum_n,
        wz=wz, wbc=wbc, wo=wo, wx=wx, conv_rep=conv_rep, xdt=xdt, dtw=dtw, w1=w1,
        w2=i["L0_ffn_W2"].transpose(1, 0, 2), b2=b2.reshape(rows_of * EXPERTS, rows_of * CH), gate_w=gate_w,
        gate_b=np.broadcast_to(i["L0_ffn_gate_b"], (P, rows_of, EXPERTS)),
        rank=np.broadcast_to(np.arange(EXPERTS, 0, -1).astype(f), (P, rows_of, EXPERTS)))
    return {n: np.ascontiguousarray(a) for n, a in arrays.items()}


def kernel(**inputs):
    import numpy as np
    import concourse.bacc as bacc
    from concourse.bass_utils import run_bass_kernel_spmd

    nc = bacc.Bacc("TRN2", target_bir_lowering=False, num_devices=1)
    arrays = layouts(np, {n: np.asarray(a) for n, a in inputs.items()})
    d = {n: nc.dram_tensor("in_" + n, a.shape, F32, kind="ExternalInput").ap() for n, a in arrays.items()}
    out = nc.dram_tensor("out", (CLIPS, TOKENS, CH), F32, kind="ExternalOutput").ap()
    scratch = [nc.dram_tensor(n, (2, rows, UNITS, TOKENS), F32, kind="Internal").ap()
               for n, rows in (("bc_scratch", 2 * NSTATE), ("delta_scratch", DIN))]
    build(nc, d, out, scratch)
    r = run_bass_kernel_spmd(nc, [{"in_" + n: a for n, a in arrays.items()}], core_ids=[0])
    return r.results[0]["out"]
```

```python
from contextlib import ExitStack

import concourse.bass as bass
from concourse import mybir

ALU = mybir.AluOpType
ACT = mybir.ActivationFunctionType
AX = mybir.AxisListType
F32 = mybir.dt.float32

P = 128
CLIPS, TOKENS, CH = 32, 375, 64
PAIRS = CLIPS // 2
TAPS = 5
DIN, NSTATE, RANK, CTAPS = 128, 16, 16, 4
ND, NN = 32, 4
DG, NG = DIN // ND, NSTATE // NN
UNITS = 4
STEPS = UNITS * DG
EXPERTS, HID = 8, 128
AHEAD = 3
LOG_MARGIN = 2.0 ** -23
CHUNKS, CT = 3, 125

COLS = {}
for _name, _n in (("tok_w", TAPS), ("tok_b", 1), ("gamma", 1), ("beta", 1), ("alpha", 1), ("conv_b", 2), ("dt_b", 2),
                  ("D", 2), ("a_log", 2 * DG * NG), ("b1", EXPERTS), ("eps_clip", 1), ("eps_ln", 1), ("one", 1)):
    COLS[_name] = (sum(n for _, n in COLS.values()), _n)
NCOLS = sum(n for _, n in COLS.values())


def wait(eng, semaphore, count):
    if not isinstance(count, int) or count > 0:
        eng.wait_ge(semaphore, count)


_ROWS = 2 * CHUNKS
EXPERT_ARRAYS = {
    "w1": [P, 2, EXPERTS, HID],
    "w2": [HID, EXPERTS, CH],
    "b2": [_ROWS * EXPERTS, _ROWS * CH],
    "gate_w": [P, 2, EXPERTS],
    "gate_b": [P, _ROWS, EXPERTS],
    "rank": [P, _ROWS, EXPERTS],
}


def load_constants(nc, ctx, d):
    shapes = {
        "cols": [P, NCOLS], "ident": [P, P], "center": [P, P], "average": [P, P],
        "sel_d": [P, DG, P], "sum_n": [P, ND],
        "wz": [P, 2, DIN], "wbc": [P, 2, 2 * NSTATE], "wo": [P, 2, 2, P],
    }
    return {n: (ctx.enter_context(nc.sbuf_tensor("c_" + n, s, F32)), d[n]) for n, s in shapes.items()}


def normalize_tokens(v, c, w, h, n, neg, steps, before):
    tile = h[:, n, :]
    column = slice(n, n + 1) if isinstance(n, int) else bass.ds(n, 1)
    alpha = c["cols"][0][:, COLS["alpha"][0]:COLS["alpha"][0] + 1]
    v.tensor_scalar(tile, tile, w["scale"][:, column], w["shift"][:, column], ALU.mult, ALU.add).then_inc(steps, 1)
    v.wait_ge(steps, before + 1)
    v.tensor_scalar(neg[:], tile, 0.0, alpha, ALU.min, ALU.mult).then_inc(steps, 1)
    v.wait_ge(steps, before + 2)
    v.scalar_tensor_tensor(tile, tile, 0.0, neg[:], ALU.max, ALU.add).then_inc(steps, 1)


def token_phase(nc, c, h, w, experts, d):
    with ExitStack() as ctx:
        def sb(name, shape, dt=F32):
            return ctx.enter_context(nc.sbuf_tensor(name, shape, dt))

        def sem(name):
            return ctx.enter_context(nc.semaphore(name))

        SLOTS = 4
        taps = ((1, 0), (0, 1), (1, 1), (0, 2), (1, 2))
        PE_TAPS = 3
        x = sb("x", [P, SLOTS, 2, TOKENS + 2])
        tap = sb("tap", [P, PE_TAPS, P])
        wx = sb("wx", [P, 2, DIN])
        conv_rep = sb("conv_rep", [P, 2, 2, DIN])
        xdt = sb("xdt", [RANK, 2, DIN])
        dtw = sb("dtw", [RANK, 2, DIN])
        stats = sb("stats", [P, PAIRS, 6])
        mv = sb("mv", [P, PAIRS, 2])
        dev = sb("dev", [P, PAIRS])
        dev2 = sb("dev2", [P, PAIRS])
        lnv = sb("lnv", [P, PAIRS])
        scale, shift = w["scale"], w["shift"]
        mean = sb("mean", [P, PAIRS])
        neg = sb("neg", [P, TOKENS])
        ps_conv = ctx.enter_context(nc.psum_tensor("ps_conv", [P, 2, 512], F32))
        ps_stat = ctx.enter_context(nc.psum_tensor("ps_stat", [P, 2, 512], F32))
        ps_wdt = ctx.enter_context(nc.psum_tensor("ps_wdt", [P, 2, 512], F32))

        consts_in = sem("consts_in")
        weights_in = sem("weights_in")
        experts_in = sem("experts_in")
        x_in = [sem(f"x_in{k}") for k in range(SLOTS)]
        x_zeroed = sem("x_zeroed")
        conv_ready = sem("conv_ready")
        tap_added = sem("tap_added")
        taps_made = sem("taps_made")
        slot_free = sem("slot_free")
        stat_done = sem("stat_done")
        agg_done = sem("agg_done")
        mean_ready = sem("mean_ready")
        dve = sem("dve")
        var_ready = sem("var_ready")
        rstd_steps = sem("rstd_steps")
        finished = sem("finished")
        wdt_ready = sem("wdt_ready")
        act_weights = sem("act_weights")
        pool_weights = sem("pool_weights")
        late = [c[n] for n in ("center", "average", "wz", "wbc", "wo", "sel_d", "sum_n")]
        late += [(wx, d["wx"]), (conv_rep, d["conv_rep"]), (xdt, d["xdt"]), (dtw, d["dtw"])]

        def col(name, k=0, rows=P):
            at = COLS[name][0] + k
            return c["cols"][0][0:rows, at:at + 1]

        block = ctx.enter_context(nc.Block())

        @block.sync
        def _(sp):
            for name in ("cols", "ident"):
                t, src = c[name]
                sp.dma_start(t[:], src).then_inc(consts_in, 16)

            def load_x(pair, k):
                sp.dma_start(x[:, k, :, 1:TOKENS + 1], d["x"][pair]).then_inc(x_in[k], 16)

            sp.wait_ge(x_zeroed, 1)
            for k in range(SLOTS):
                load_x(k, k)
            for t, src in late:
                sp.dma_start(t[:], src).then_inc(weights_in, 16)
            with sp.Fori(1, PAIRS // SLOTS) as i:
                for k in range(SLOTS):
                    pair = SLOTS * i + k
                    sp.wait_ge(tap_added, 2 * (pair - SLOTS) + 2)
                    load_x(pair, k)
            for name, t in experts.items():
                sp.dma_start(t[:], d[name]).then_inc(experts_in, 16)
            sp.wait_ge(experts_in, 16 * len(experts))

        @block.scalar
        def _(act):
            act.preload_act_table_set("natural_log_exp_and_others")
            act.sem_inc(slot_free, 2)
            act.wait_ge(consts_in, 32)
            with act.Fori(0, PAIRS // 2) as i:
                for k in range(2):
                    act.wait_ge(conv_ready, 2 * i + k + 1)
                    act.activation(h[:, 2 * i + k, :], ps_conv[:, k, 0:TOKENS], ACT.Identity,
                                   bias=col("tok_b")).then_inc(slot_free, 1)
            act.wait_ge(weights_in, 16 * len(late))
            act.activation(w["decay"][:, 0, :], col2(c, "a_log"), ACT.Exp).then_inc(act_weights, 1)
            act.activation(c["wo"][0][:], c["wo"][0][:], ACT.Copy, scale=0.5).then_inc(act_weights, 1)
            act.wait_ge(wdt_ready, 1)
            act.activation(w["wdt"][:], ps_wdt[:, :, 0:DIN], ACT.Copy).then_inc(act_weights, 1)
            act.wait_ge(var_ready, 1)
            act.activation(lnv[:], ps_stat[:, 1, 0:PAIRS], ACT.Ln, bias=col("eps_clip")).then_inc(rstd_steps, 1)
            act.wait_ge(rstd_steps, 1)
            act.activation(scale[:], lnv[:], ACT.Exp, scale=-0.5).then_inc(rstd_steps, 1)
            act.wait_ge(act_weights, 3)

        @block.tensor
        def _(pe):
            pe.wait_ge(taps_made, PE_TAPS)
            with pe.Fori(0, PAIRS // SLOTS) as i:
                for k in range(SLOTS):
                    pe.wait_ge(x_in[k], 16 * i + 16)
                    pe.wait_ge(slot_free, SLOTS * i + k + 1)
                    for t in range(PE_TAPS):
                        parity, at = taps[t]
                        mm = pe.matmul(ps_conv[:, k % 2, 0:TOKENS], tap[:, t, :], x[:, k, parity, at:at + TOKENS],
                                       start=(t == 0), stop=(t == PE_TAPS - 1))
                    mm.then_inc(conv_ready, 1)
            pe.wait_ge(weights_in, 16 * len(late))
            for r in range(2):
                mm = pe.matmul(ps_wdt[:, r, 0:DIN], xdt[:, r, :], dtw[:, r, :], start=True, stop=True)
            mm.then_inc(wdt_ready, 1)
            pe.wait_ge(agg_done, PAIRS)
            pe.wait_ge(dve, 1)
            pe.matmul(ps_stat[:, 0, 0:PAIRS], c["average"][0][:], mean[:], start=True, stop=True).then_inc(mean_ready, 1)
            pe.wait_ge(dve, 4)
            pe.matmul(ps_stat[:, 1, 0:PAIRS], c["average"][0][:], dev2[:], start=True, stop=True).then_inc(var_ready, 1)

        @block.vector
        def _(v):
            v.memset(x[:, :, :, 0:TOKENS + 2:TOKENS + 1], 0.0).then_inc(x_zeroed, 1)
            v.wait_ge(consts_in, 32)
            for t in range(PE_TAPS):
                v.tensor_scalar(tap[:, t, :], c["ident"][0][:], col("tok_w", t), None, ALU.mult).then_inc(taps_made, 1)
            with v.Fori(0, PAIRS // SLOTS) as i:
                for k in range(SLOTS):
                    n = SLOTS * i + k
                    v.wait_ge(slot_free, n + 3)
                    for t in range(PE_TAPS, TAPS):
                        parity, at = taps[t]
                        v.scalar_tensor_tensor(h[:, n, :], x[:, k, parity, at:at + TOKENS], col("tok_w", t), h[:, n, :],
                                               ALU.mult, ALU.add).then_inc(tap_added, 1)
                        v.wait_ge(tap_added, 2 * n + t - PE_TAPS + 1)
                    v.bn_stats(stats[:, n, :], h[:, n, :]).then_inc(stat_done, 1)
            v.wait_ge(stat_done, PAIRS)
            for n in range(PAIRS):
                v.bn_aggr(mv[:, n, :], stats[:, n, :]).then_inc(agg_done, 1)
            v.wait_ge(agg_done, PAIRS)
            v.tensor_copy(mean[:], mv[:, :, 0]).then_inc(dve, 1)
            v.wait_ge(mean_ready, 1)
            v.wait_ge(dve, 1)
            v.scalar_tensor_tensor(dev[:], ps_stat[:, 0, 0:PAIRS], -1.0, mean[:], ALU.mult, ALU.add).then_inc(dve, 1)
            v.wait_ge(dve, 2)
            v.tensor_tensor(dev2[:], dev[:], dev[:], ALU.mult).then_inc(dve, 1)
            v.wait_ge(dve, 3)
            v.tensor_tensor(dev2[:], dev2[:], mv[:, :, 1], ALU.add).then_inc(dve, 1)
            v.wait_ge(rstd_steps, 2)
            v.tensor_scalar(scale[:], scale[:], col("gamma"), None, ALU.mult).then_inc(dve, 1)
            v.wait_ge(dve, 5)
            v.scalar_tensor_tensor(shift[:], ps_stat[:, 0, 0:PAIRS], -1.0, scale[:], ALU.mult, ALU.mult).then_inc(dve, 1)
            v.wait_ge(dve, 6)
            v.tensor_scalar(shift[:], shift[:], col("beta"), None, ALU.add).then_inc(dve, 1)
            v.wait_ge(dve, 7)
            normalize_tokens(v, c, w, h, 0, neg, finished, 0)
            v.wait_ge(finished, 3)

        @block.gpsimd
        def _(g):
            g.wait_ge(weights_in, 16 * len(late))
            for r in range(2):
                src = wx[:, r, :].unsqueeze(1).to_broadcast([P, 2, DIN])
                g.tensor_tensor(w["wk"][:, r, :, :], src, conv_rep[:, r, :, :], ALU.mult).then_inc(pool_weights, 1)
            g.wait_ge(consts_in, 32)
            for r in range(2):
                g.tensor_scalar(w["skip"][:, r, :], c["ident"][0][:], col("D", r), None, ALU.mult).then_inc(pool_weights, 1)
            g.wait_ge(act_weights, 1)
            g.tensor_scalar(w["decay"][:, 1, :], w["decay"][:, 0, :], -1.0, None, ALU.mult).then_inc(pool_weights, 1)
            g.wait_ge(pool_weights, 5)


def col2(c, name):
    at, n = COLS[name]
    return c["cols"][0][:, at:at + n]


def stage_jobs(s, has_next, has_before):
    jobs = []
    if has_next:
        jobs += {0: ["cen", "var"], 3: ["x0", "z0"], 4: ["x1", "z1"], 5: ["x2", "z2"], 6: ["x3", "z3"],
                 7: ["dt0", "dt1"], 8: ["dt2", "dt3"], 9: ["bc0"], 10: ["bc1"], 11: ["bc2"], 12: ["bc3"]}.get(s, [])
    if s == 2 and has_before:
        jobs.append("out1")
    if s == 11:
        jobs.append("out0")
    return jobs


def pair_jobs(has_next, has_before):
    return [j for s in range(STEPS) for j in stage_jobs(s, has_next, has_before)]


PROLOGUE = [j for j in pair_jobs(True, False) if j != "out0"]
N_PRO, N_FIRST, N_MID = len(PROLOGUE), len(pair_jobs(True, False)), len(pair_jobs(True, True))


class Jobs:

    def __init__(self, names, base, parity):
        self.names, self.base, self.parity = names, base, parity

    def number(self, job):
        return self.base + self.names.index(job)

    def bank(self, job):
        return (self.parity + self.names.index(job)) % 2


def jobs_of(pair, has_next, has_before):
    assert N_MID % 2 == 0
    if not has_before:
        return Jobs(pair_jobs(has_next, False), N_PRO, N_PRO % 2)
    return Jobs(pair_jobs(has_next, True), N_PRO + N_FIRST + N_MID * (pair - 1), (N_PRO + N_FIRST) % 2)


PROLOGUE_JOBS = Jobs(PROLOGUE, 0, 0)
_before_tail = N_PRO + N_FIRST + N_MID * (PAIRS - 2) + len(pair_jobs(False, True))
TAIL_JOBS = Jobs(["out1"], _before_tail, _before_tail % 2)


def mamba_phase(nc, c, h, w, bc_dram, dl_dram):
    with ExitStack() as ctx:
        def sb(name, shape, dt=F32):
            return ctx.enter_context(nc.sbuf_tensor(name, shape, dt))

        def ps(name, shape):
            return ctx.enter_context(nc.psum_tensor(name, shape, F32))

        def sem(name):
            return ctx.enter_context(nc.semaphore("m_" + name))

        T = TOKENS
        PAD = CTAPS - 1
        cen = sb("cen", [P, T])
        sq = sb("sq", [P, T])
        rstd = sb("rstd", [P, T])
        un = sb("un", [P, T + 2 * PAD])
        two = sb("two", [P, 2, T + 2 * PAD])
        xs = sb("xs", [P, 2, UNITS, T])
        sz = sb("sz", [P, 2, UNITS, T])
        dl = sb("dl", [P, UNITS, T])
        du = sb("du", [P, 2, UNITS, T])
        pre = sb("pre", [P, UNITS, T])
        tmp = sb("tmp", [P, UNITS, T])
        bc = sb("bc", [2 * NSTATE, UNITS, T])
        brep = sb("brep", [P, 2, NG, T])
        crep = sb("crep", [P, 2, NG, T])
        drep = sb("drep", [P, 2, DG, T])
        dec = sb("dec", [P, 4, NG * T + 1])
        st = sb("st", [P, 4, NG, T])
        yz = sb("yz", [P, 2, T])
        res = sb("res", [P, 2, T])
        ps_du = ps("ps_du", [P, 2, 512])
        ps_y = ps("ps_y", [P, 512])
        ps_job = ps("ps_job", [P, 2, 512])
        ps_b = ps("ps_b", [P, 3 * 512])

        zeroed = sem("zeroed")
        tokens = sem("tokens")
        job_ready = sem("job_ready")
        job_taken = sem("job_taken")
        sq_ready = sem("sq_ready")
        rstd_ready = sem("rstd_ready")
        un_ready = sem("un_ready")
        two_in = sem("two_in")
        silu_ready = sem("silu_ready")
        softplus = sem("softplus")
        square_ready = sem("square_ready")
        delta_step = sem("delta_step")
        dl_ready = sem("dl_ready")
        dl_out = sem("dl_out")
        bc_out = sem("bc_out")
        du_ready = sem("du_ready")
        d_in = [sem("d_in0"), sem("d_in1")]
        b_in = [sem("b_in0"), sem("b_in1")]
        c_in = [sem("c_in0"), sem("c_in1")]
        du_rep = sem("du_rep")
        decay_ready = sem("decay_ready")
        drive_ready = sem("drive_ready")
        state_ready = sem("state_ready")
        weighted = sem("weighted")
        summed = sem("summed")
        gated = sem("gated")
        added = sem("added")

        def const(name):
            return c[name][0]

        def col(name, k=0):
            at = COLS[name][0] + k
            return c["cols"][0][:, at:at + 1]

        def decay_col(r, g, n):
            at = r * DG * NG + g * NG + n
            return w["decay"][:, 1, at:at + 1]

        def seg(r):
            return slice(1, T) if r == 0 else slice(0, T - 1)

        def arrivals(q, u):
            return 64 * (UNITS // 2 * q + u // 2 + 1)

        def run_pairs(prologue, pair_body, tail, engine):
            prologue()
            pair_body(0, 0, jobs_of(0, True, False), True, False)
            with engine.Fori(0, (PAIRS - 2) // 2) as i:
                for k in range(2):
                    q = 2 * i + 1 + k
                    pair_body(q, (1 + k) % 2, jobs_of(q, True, True), True, True)
            q = PAIRS - 1
            pair_body(q, q % 2, jobs_of(q, False, True), False, True)
            tail()

        block = ctx.enter_context(nc.Block())
        flat = "p a b -> p (a b)"

        @block.sync
        def _(sp):
            def stack(q):
                sp.wait_ge(un_ready, q + 1)
                for b in range(2):
                    rows = un[CH * b:CH * b + CH]
                    sp.dma_start(two[0:CH, b, :], rows).then_inc(two_in, 16)
                    sp.dma_start(two[CH:P, b, 0:T + 2 * PAD - 2], rows[:, 2:]).then_inc(two_in, 16)

            def write(q, k):
                sp.wait_ge(dl_ready, q + 1)
                sp.dma_start(dl_dram[k], dl[:]).then_inc(dl_out, 16)
                sp.wait_ge(job_taken, job_numbers(q).number("bc3") + 1)
                sp.dma_start(bc_dram[k], bc[:]).then_inc(bc_out, 16)

            numbers = {}

            def job_numbers(q):
                return numbers["of"]

            def read_delta(q, k, u):
                if u == 0:
                    sp.wait_ge(dl_out, 16 * (q + 1))
                wait(sp, decay_ready, DG * (UNITS * q + u - 1))
                for n in range(NN):
                    rows = slice(ND * n, ND * n + ND)
                    sp.dma_start(drep[rows, u % 2], dl_dram[k, :, u, :].rearrange("(g d) t -> d g t", g=DG))\
                      .then_inc(d_in[u % 2], 16)

            def read_states(q, k, u, first, buf, arrived, used, count):
                wait(sp, used, count * DG * (UNITS * q + u - 1))
                if u == 0:
                    sp.wait_ge(bc_out, 16 * (q + 1))
                for n in range(NN):
                    src = bc_dram[k, first + n:first + NSTATE:NN, u, :].unsqueeze(0).to_broadcast([ND, NG, T])
                    sp.dma_start(buf[ND * n:ND * n + ND, u % 2], src).then_inc(arrived[u % 2], 16)

            def read_b(q, k, u):
                read_states(q, k, u, 0, brep, b_in, drive_ready, 2)

            def read_c(q, k, u):
                read_states(q, k, u, NSTATE, crep, c_in, weighted, 1)

            def prologue():
                numbers["of"] = PROLOGUE_JOBS
                stack(0)
                write(0, 0)
                for read in (read_delta, read_b, read_c):
                    read(0, 0, 0)

            def pair_body(q, k, jobs, has_next, has_before):
                numbers["of"] = jobs
                read_delta(q, k, 1)
                read_b(q, k, 1)
                if has_next:
                    stack(q + 1)
                read_c(q, k, 1)
                for u in (2, 3):
                    for read in (read_delta, read_b, read_c):
                        read(q, k, u)
                if has_next:
                    write(q + 1, 1 - k)
                    for read in (read_delta, read_b, read_c):
                        read(q + 1, 1 - k, 0)

            run_pairs(prologue, pair_body, lambda: None, sp)

        @block.tensor
        def _(pe):
            def project(jobs, name, q, kq):
                kind, u = name[:-1], ord(name[-1]) - ord("0")
                b, r = u // 2, u % 2
                if name == "var":
                    pe.wait_ge(sq_ready, q + 1)
                elif kind in ("x", "z"):
                    pe.wait_ge(two_in, 64 * (q + 1))
                elif kind in ("dt", "bc"):
                    pe.wait_ge(silu_ready, 2 * q + 1)
                elif kind == "out":
                    b = u
                    pe.wait_ge(gated, UNITS * q + 2 * b + 2)
                wait(pe, job_taken, jobs.number(name) - 1)
                out = ps_job[:, jobs.bank(name), 0:T]
                if name == "cen":
                    products = [(const("center")[:], h[:, q, :])]
                elif name == "var":
                    products = [(const("average")[:], sq[:])]
                elif kind == "x":
                    starts = (0, 1) if r == 0 else (PAD + 1, PAD)
                    products = [(w["wk"][:, r, i, :], two[:, b, at:at + T]) for i, at in enumerate(starts)]
                elif kind == "z":
                    products = [(const("wz")[:, r, :], two[:, b, PAD:PAD + T])]
                elif kind == "dt":
                    products = [(w["wdt"][:, r, :], xs[:, kq, u, :])]
                elif kind == "bc":
                    out = out[0:2 * NSTATE]
                    products = [(const("wbc")[:, r, :], xs[:, kq, u, :])]
                else:
                    products = [(const("wo")[:, r, b, :], yz[:, r, :]) for r in range(2)]
                for i, (weight, moving) in enumerate(products):
                    mm = pe.matmul(out, weight, moving, start=(i == 0), stop=(i == len(products) - 1))
                mm.then_inc(job_ready, 1)

            def replicate_du(step, q, k, s):
                u, g = divmod(s, DG)
                pe.wait_ge(du_ready, q + 1)
                wait(pe, drive_ready, 2 * (step - 1))
                pe.matmul(ps_du[:, s % 2, 0:T], const("sel_d")[:, g, :], du[:, k, u, :], start=True,
                          stop=True).then_inc(du_rep, 1)

            def sum_states(step, unit, k, s):
                u, g = divmod(s, DG)
                if g == 1:
                    wait(pe, gated, unit)
                    pe.matmul(ps_y[:, 0:T], w["skip"][:, u % 2, :], xs[:, k, u, :], start=True, stop=False,
                              skip_group_check=True)
                pe.wait_ge(weighted, step + 1)
                for n in range(NG):
                    for back in (1, 0):
                        rows = slice(ND * (g - back), ND * (g - back) + ND)
                        mm = pe.matmul(ps_y[rows, 0:T], const("sum_n")[:], st[:, (s - back) % 4, n, :], start=False,
                                       stop=(n == NG - 1), skip_group_check=True)
                mm.then_inc(summed, 2)

            def prologue():
                pe.wait_ge(zeroed, 1)
                for name in PROLOGUE:
                    project(PROLOGUE_JOBS, name, 0, 0)
                pe.wait_ge(tokens, 3 * (PAIRS - 1))
                replicate_du(0, 0, 0, 0)

            def pair_body(q, k, jobs, has_next, has_before):
                for s in range(STEPS):
                    step = STEPS * q + s
                    if s + 1 < STEPS:
                        replicate_du(step + 1, q, k, s + 1)
                    elif has_next:
                        replicate_du(step + 1, q + 1, 1 - k, 0)
                    if s > 1 and s % 2 == 1:
                        sum_states(step - 2, UNITS * q + (s - 2) // DG, k, s - 2)
                    elif s == 1 and has_before:
                        sum_states(step - 2, UNITS * q - 1, 1 - k, STEPS - 1)
                    for name in stage_jobs(s, has_next, has_before):
                        if name == "out1":
                            project(jobs, name, q - 1, None)
                        elif name == "out0":
                            project(jobs, name, q, None)
                        else:
                            project(jobs, name, q + 1, 1 - k)

            def tail():
                q = PAIRS - 1
                sum_states(STEPS * q + STEPS - 1, UNITS * q + UNITS - 1, q % 2, STEPS - 1)
                project(TAIL_JOBS, "out1", q, None)

            run_pairs(prologue, pair_body, tail, pe)

        @block.scalar
        def _(act):
            def take(jobs, name, out, func=ACT.Copy, bias=None):
                act.wait_ge(job_ready, jobs.number(name) + 1)
                bank = ps_job[0:out.shape[0], jobs.bank(name), 0:T]
                if bias is None:
                    act.activation(out, bank, func).then_inc(job_taken, 1)
                else:
                    act.activation(out, bank, func, bias=bias).then_inc(job_taken, 1)

            def do_job(jobs, name, q, k):
                kind, u = name[:-1], ord(name[-1]) - ord("0")
                if name == "cen":
                    take(jobs, name, cen[:])
                    act.wait_ge(job_taken, jobs.number(name) + 1)
                    act.activation(sq[:], cen[:], ACT.Square).then_inc(sq_ready, 1)
                elif name == "var":
                    take(jobs, name, sq[:], ACT.Ln, col("eps_ln"))
                    act.wait_ge(job_taken, jobs.number(name) + 1)
                    act.activation(rstd[:], sq[:], ACT.Exp, scale=-0.5).then_inc(rstd_ready, 1)
                elif kind == "x":
                    take(jobs, name, xs[:, k, u, :], ACT.Identity, col("conv_b", u % 2))
                elif kind == "z":
                    if u == 0:
                        wait(act, gated, UNITS * (q - 1))
                    take(jobs, name, sz[:, k, u, :])
                elif kind == "dt":
                    take(jobs, name, pre[:, u, :], ACT.Identity, col("dt_b", u % 2))
                elif kind == "bc":
                    if u == 0:
                        wait(act, bc_out, 16 * q)
                    take(jobs, name, bc[:, u, :])
                elif kind == "out":
                    wait(act, added, 2 * q + u - 1)
                    take(jobs, name, res[:, u, :])

            def silus(jobs, k):
                act.preload_act_table_set("silu_and_others")
                act.wait_ge(job_taken, jobs.number("z3") + 1)
                for t in (xs, sz):
                    act.activation(t[:, k], t[:, k], ACT.Silu).then_inc(silu_ready, 1)
                act.preload_act_table_set("natural_log_exp_and_others")

            def softplus_steps(jobs, q, k):
                act.wait_ge(job_taken, jobs.number("dt3") + 1)
                act.activation(tmp[:], pre[:], ACT.Abs).then_inc(softplus, 1)
                act.wait_ge(softplus, 3 * q + 1)
                act.activation(tmp[:], tmp[:], ACT.Exp, scale=-1.0).then_inc(softplus, 1)
                act.wait_ge(softplus, 3 * q + 2)
                act.activation(du[:, k], tmp[:], ACT.Square).then_inc(square_ready, 1)
                wait(act, dl_out, 16 * q)
                act.activation(dl[:], tmp[:], ACT.Ln, bias=col("one")).then_inc(softplus, 1)

            def decays(step, q, s):
                u, g = divmod(s, DG)
                r = u % 2
                act.wait_ge(d_in[u % 2], arrivals(q, u))
                wait(act, state_ready, 2 * (step - 3))
                for n in range(NG):
                    ins = act.activation(dec[:, s % 4, n * T + 1:n * T + T], drep[:, u % 2, g, seg(r)], ACT.Exp,
                                         scale=decay_col(r, g, n))
                ins.then_inc(decay_ready, 1)

            def prologue():
                for name in PROLOGUE:
                    do_job(PROLOGUE_JOBS, name, 0, 0)
                    if name == "z3":
                        silus(PROLOGUE_JOBS, 0)
                    if name == "dt3":
                        softplus_steps(PROLOGUE_JOBS, 0, 0)
                act.wait_ge(zeroed, 1)
                for s in range(AHEAD):
                    decays(s, 0, s)

            def pair_body(q, k, jobs, has_next, has_before):
                for s in range(STEPS):
                    step = STEPS * q + s
                    if s + AHEAD < STEPS:
                        decays(step + AHEAD, q, s + AHEAD)
                    elif has_next:
                        decays(step + AHEAD, q + 1, s + AHEAD - STEPS)
                    for name in stage_jobs(s, has_next, has_before):
                        if name == "out1":
                            do_job(jobs, name, q - 1, None)
                        elif name == "out0":
                            do_job(jobs, name, q, None)
                        else:
                            do_job(jobs, name, q + 1, 1 - k)
                    if has_next and s == 6:
                        silus(jobs, 1 - k)
                    if has_next and s == 8:
                        softplus_steps(jobs, q + 1, 1 - k)

            def tail():
                do_job(TAIL_JOBS, "out1", PAIRS - 1, None)

            run_pairs(prologue, pair_body, tail, act)

        @block.vector
        def _(v):
            def normalize(q):
                v.wait_ge(rstd_ready, q + 1)
                wait(v, two_in, 64 * q)
                v.tensor_tensor(un[:, PAD:PAD + T], cen[:], rstd[:], ALU.mult).then_inc(un_ready, 1)

            def delta(q, k):
                d_, p_ = dl[:].rearrange(flat), tmp[:].rearrange(flat)
                v.wait_ge(softplus, 3 * q + 3)
                v.wait_ge(square_ready, q + 1)
                v.scalar_tensor_tensor(p_, du[:, k].rearrange(flat), -0.5, p_, ALU.mult, ALU.add).then_inc(delta_step, 1)
                v.wait_ge(delta_step, 2 * q + 1)
                v.scalar_tensor_tensor(d_, d_, -LOG_MARGIN, p_, ALU.add, ALU.max).then_inc(delta_step, 1)
                v.wait_ge(delta_step, 2 * q + 2)
                v.scalar_tensor_tensor(d_, pre[:].rearrange(flat), 0.0, d_, ALU.max, ALU.add).then_inc(dl_ready, 1)

            def scan(step, q, s):
                u, g = divmod(s, DG)
                r = u % 2
                v.wait_ge(du_rep, step + 1)
                if g == 0:
                    v.wait_ge(b_in[u % 2], arrivals(q, u))
                half = NG // 2 * T
                rows = "p (a b) -> p a b"
                for i in range(2):
                    wait(v, state_ready, 2 * step - 1 + i)
                    part = slice(i * half, i * half + half)
                    v.tensor_tensor(ps_b[:, part].rearrange(rows, b=T),
                                    ps_du[:, s % 2, 0:T].unsqueeze(1).to_broadcast([P, NG // 2, T]),
                                    brep[:, u % 2, NG // 2 * i:NG // 2 * i + NG // 2], ALU.mult).then_inc(drive_ready, 1)
                v.wait_ge(decay_ready, step + 1)
                wait(v, summed, step - 3)
                for i in range(2):
                    v.wait_ge(drive_ready, 2 * step + 1 + i)
                    part = slice(i * half, i * half + half)
                    order = slice(None) if r == 0 else slice(None, None, -1)
                    v.tensor_tensor_scan(st[:, s % 4].rearrange(flat)[:, part][:, order],
                                         dec[:, s % 4, r + i * half:r + i * half + half][:, order],
                                         ps_b[:, part][:, order], 0.0, ALU.mult, ALU.add).then_inc(state_ready, 1)

            def gate(unit, k, u, last_read):
                v.wait_ge(summed, DG * unit + DG)
                if last_read is not None:
                    v.wait_ge(job_ready, last_read)
                v.tensor_tensor(yz[:, u % 2, :], ps_y[:, 0:T], sz[:, k, u, :], ALU.mult).then_inc(gated, 1)

            def prologue():
                v.memset(dec[:, :, 0:NG * T + 1:T], 0.0)
                v.memset(un[:, 0:PAD], 0.0)
                v.memset(un[:, PAD + T:], 0.0).then_inc(zeroed, 1)
                v.wait_ge(zeroed, 1)
                normalize(0)
                with v.Fori(1, PAIRS) as n:
                    normalize_tokens(v, c, w, h, n, st[:, 0, 0, :], tokens, 3 * (n - 1))
                    v.wait_ge(tokens, 3 * n)
                delta(0, 0)

            def pair_body(q, k, jobs, has_next, has_before):
                for s in range(STEPS):
                    step = STEPS * q + s
                    u = s // DG
                    scan(step, q, s)
                    if s % DG == 1:
                        if u > 0:
                            read = {1: "out1" if has_before else None, 3: "out0"}.get(u)
                            gate(UNITS * q + u - 1, k, u - 1, None if read is None else jobs.number(read) + 1)
                        elif has_before:
                            gate(UNITS * q - 1, 1 - k, UNITS - 1, None)
                    if has_next and s == 1:
                        normalize(q + 1)
                    if has_next and s == 11:
                        delta(q + 1, 1 - k)

            def tail():
                q = PAIRS - 1
                gate(UNITS * q + UNITS - 1, q % 2, UNITS - 1, None)

            run_pairs(prologue, pair_body, tail, v)

        @block.gpsimd
        def _(g):
            def drive_input(q, k):
                g.wait_ge(dl_ready, q + 1)
                g.wait_ge(silu_ready, 2 * q + 1)
                g.tensor_tensor(du[:, k], dl[:], xs[:, k], ALU.mult).then_inc(du_ready, 1)

            def weight_states(step, q, s):
                u = s // DG
                g.wait_ge(c_in[u % 2], arrivals(q, u))
                g.wait_ge(state_ready, 2 * step + 2)
                g.tensor_tensor(st[:, s % 4], st[:, s % 4], crep[:, u % 2], ALU.mult).then_inc(weighted, 1)

            def add(q, b):
                g.tensor_tensor(h[:, q, :], h[:, q, :], res[:, b, :], ALU.add).then_inc(added, 1)

            def prologue():
                drive_input(0, 0)

            def pair_body(q, k, jobs, has_next, has_before):
                for s in range(STEPS):
                    b = {3: 1 if has_before else None, 12: 0}.get(s)
                    if b is not None:
                        g.wait_ge(job_taken, jobs.number(f"out{b}") + 1)
                    weight_states(STEPS * q + s, q, s)
                    if b is not None:
                        add(q - b, b)
                    if has_next and s == 11:
                        drive_input(q + 1, 1 - k)

            def tail():
                g.wait_ge(job_taken, TAIL_JOBS.base + 1)
                add(PAIRS - 1, 1)
                g.wait_ge(added, 2 * PAIRS)

            run_pairs(prologue, pair_body, tail, g)


def expert_phase(nc, c, h, experts, out):
    with ExitStack() as ctx:
        def sb(name, shape):
            return ctx.enter_context(nc.sbuf_tensor(name, shape, F32))

        def ps(name, shape):
            return ctx.enter_context(nc.psum_tensor(name, shape, F32))

        def sem(name):
            return ctx.enter_context(nc.semaphore("e_" + name))

        T, E, R = TOKENS, EXPERTS, 2 * CHUNKS
        w1, w2, b2, gate_w, gate_b, rank = (experts[n] for n in EXPERT_ARRAYS)
        cen = sb("cen2", [P, T])
        sq = sb("sq2", [P, T])
        rstd = sb("rstd2", [P, T])
        un = sb("un2", [P, 2, T])
        hc = sb("hc", [P, T])
        act_h = sb("act_h", [P, 2, E, T])
        lg = sb("lg", [CT, R, E])
        pr = sb("pr", [CT, R, E])
        hit = sb("hit", [CT, R, E])
        one1 = sb("one1", [CT, R, E])
        one2 = sb("one2", [CT, R, E])
        mx = sb("mx", [CT, R])
        cw = sb("cw", [CT, 2, R, E])
        cwt = sb("cwt", [R * E, CT])
        prod = sb("prod", [CT, 2, E, CH])
        red = sb("red", [CT, 2, R, CH])
        tok = sb("tok", [CT, 2, R, CH])
        ps_h = ps("ps_h", [P, 4, 512])
        ps_e = ps("ps_e", [P, 2, 512])
        ps_t = ps("ps_t", [P, 512])
        ps_n = ps("ps_n", [P, 512])
        ps_logits = ps_t[0:CT, R * CH:R * CH + R * E]
        ps_cwt = ps_n[0:R * E, T:T + CT]

        cen_ready = sem("cen_ready")
        cen_taken = sem("cen_taken")
        sq_ready = sem("sq_ready")
        var_ready = sem("var_ready")
        var_taken = sem("var_taken")
        rstd_ready = sem("rstd_ready")
        un_ready = sem("un_ready")
        logits_ready = sem("logits_ready")
        shifted = sem("shifted")
        exps_ready = sem("exps_ready")
        dve = sem("dve")
        cw_ready = sem("cw_ready")
        cwt_ready = sem("cwt_ready")
        cwt_taken = sem("cwt_taken")
        hc_ready = sem("hc_ready")
        base_ready = sem("base_ready")
        base_taken = sem("base_taken")
        hid_ready = sem("hid_ready")
        hid_taken = sem("hid_taken")
        out_ready = sem("out_ready")
        out_taken = sem("out_taken")
        reduced = sem("reduced")
        finished = sem("finished")
        stored = [sem("stored0"), sem("stored1")]

        def const(name):
            return c[name][0]

        def col(name, k=0):
            at = COLS[name][0] + k
            return c["cols"][0][:, at:at + 1]

        GATE_STEPS = 17
        AFTER = ({1: (0,), 4: (1,), 6: (2,)}, {2: (0,1,2)})

        def run_pairs(prologue, pair_body, tail, engine):
            def body(q, k, turn, ahead=2, has_before=True):
                pair_body(q, k, ahead > 0, ahead > 1, has_before, turn)

            prologue()
            body(0, 0, 0, has_before=False)
            with engine.Fori(0, (PAIRS - 4) // 2) as i:
                for k in range(2):
                    body(2 * i + 1 + k, (1 + k) % 2, i + 1)
            for q in range(PAIRS - 3, PAIRS):
                body(q, q % 2, (q + 1) // 2, PAIRS - 1 - q)
            tail()

        block = ctx.enter_context(nc.Block())

        @block.sync
        def _(sp):
            def prologue():
                pass

            def pair_body(q, k, has_next, has_two, has_before, turn):
                if has_before:
                    store(q - 1, 1 - k)

            def store(q, k):
                sp.wait_ge(finished, q + 1)
                for b in range(2):
                    sp.dma_start(out[2 * q + b].rearrange("(p c) n -> p c n", c=CHUNKS),
                                 tok[:, k, CHUNKS * b:CHUNKS * b + CHUNKS, :]).then_inc(stored[k], 16)

            run_pairs(prologue, pair_body, lambda: store(PAIRS - 1, (PAIRS - 1) % 2), sp)
            for k in range(2):
                sp.wait_ge(stored[k], 16 * 2 * (PAIRS // 2))

        @block.tensor
        def _(pe):
            def center(q):
                wait(pe, cen_taken, q)
                wait(pe, cwt_taken, q - 1)
                pe.matmul(ps_n[:, 0:T], const("center")[:], h[:, q, :], start=True, stop=True).then_inc(cen_ready, 1)

            def variance(q):
                pe.wait_ge(sq_ready, q + 1)
                pe.wait_ge(cen_taken, q + 1)
                pe.matmul(ps_n[:, 0:T], const("average")[:], sq[:], start=True, stop=True).then_inc(var_ready, 1)

            def logits(q, k):
                pe.wait_ge(un_ready, q + 1)
                wait(pe, shifted, q)
                wait(pe, base_taken, q - 1)
                for b in range(2):
                    for ch in range(CHUNKS):
                        at = (b * CHUNKS + ch) * E
                        mm = pe.matmul(ps_logits[:, at:at + E], un[:, k, ch:T:CHUNKS], gate_w[:, b, :], start=True, stop=True)
                mm.then_inc(logits_ready, 1)

            def turn_weights(q, k):
                pe.wait_ge(cw_ready, q + 1)
                pe.matmul(ps_cwt, cw[:, k].rearrange("p a b -> p (a b)"), const("ident")[0:CT, 0:CT],
                          start=True, stop=True).then_inc(cwt_ready, 1)

            def base(q, with_next):
                pe.wait_ge(shifted, q + 1 + with_next)
                pe.wait_ge(cwt_taken, q + 1)
                pe.wait_ge(hc_ready, q + 1)
                wait(pe, base_taken, q)
                pe.matmul(ps_t[0:CT, 0:R * CH], cwt[:], b2[:], start=True, stop=False, skip_group_check=True)
                rows = ps_t[0:CT, 0:R * CH].rearrange("p (b c n) -> p b c n", b=2, c=CHUNKS)
                for ch in range(CHUNKS):
                    mm = pe.matmul(rows[:, :, ch, :], hc[:, ch:T:CHUNKS], const("ident")[:], start=False,
                                   stop=(ch == CHUNKS - 1), skip_group_check=True)
                mm.then_inc(base_ready, 1)

            def hidden(q, k, b, e):
                n = (2 * q + b) * E + e
                wait(pe, hid_taken, n - 3)
                pe.matmul(ps_h[:, e % 4, 0:T], w1[:, b, e, :], un[:, k, :], start=True, stop=True).then_inc(hid_ready, 1)

            def experts_out(q, b, ch):
                n = (2 * q + b) * CHUNKS + ch
                pe.wait_ge(hid_taken, (2 * q + b) * E + E)
                wait(pe, out_taken, n - 1)
                for e in range(E):
                    mm = pe.matmul(ps_e[0:CT, (b * CHUNKS + ch) % 2, e * CH:e * CH + CH], act_h[:, b, e, ch:T:CHUNKS],
                                   w2[:, e, :], start=True, stop=True)
                mm.then_inc(out_ready, 1)

            def prologue():
                center(0)
                variance(0)
                logits(0, 0)
                center(1)
                variance(1)

            def pair_body(q, k, has_next, has_two, has_before, turn):
                for b in range(2):
                    for e in range(E):
                        hidden(q, k, b, e)
                        if b or has_before:
                            for ch in AFTER[b].get(e, ()):
                                experts_out(q if b else q - 1, 1 - b, ch)
                        if has_next and (b, e) == (0, 2):
                            logits(q + 1, 1 - k)
                        if has_two and (b, e) == (0, 4):
                            center(q + 2)
                        if has_two and (b, e) == (0, 6):
                            variance(q + 2)
                        if (b, e) == (0, 2):
                            turn_weights(q, k)
                        if (b, e) == (0, 7):
                            base(q, has_next)

            def tail():
                for ch in range(CHUNKS):
                    experts_out(PAIRS - 1, 1, ch)

            run_pairs(prologue, pair_body, tail, pe)

        @block.scalar
        def _(act):
            def squares(q):
                act.wait_ge(cen_ready, q + 1)
                wait(act, un_ready, q)
                act.activation(cen[:], ps_n[:, 0:T], ACT.Copy).then_inc(cen_taken, 1)
                act.wait_ge(cen_taken, q + 1)
                wait(act, rstd_ready, q)
                act.activation(sq[:], cen[:], ACT.Square).then_inc(sq_ready, 1)

            def inverse_deviation(q):
                act.wait_ge(var_ready, q + 1)
                act.activation(sq[:], ps_n[:, 0:T], ACT.Ln, bias=col("eps_ln")).then_inc(var_taken, 1)
                act.wait_ge(var_taken, q + 1)
                act.activation(rstd[:], sq[:], ACT.Exp, scale=-0.5).then_inc(rstd_ready, 1)

            def exps(q):
                act.wait_ge(shifted, q + 1)
                act.activation(pr[:], lg[:], ACT.Exp).then_inc(exps_ready, 1)

            def natural_window(q, with_deviation=True):
                act.preload_act_table_set("natural_log_exp_and_others")
                if with_deviation:
                    inverse_deviation(q + 1)
                exps(q)
                act.preload_act_table_set("gelu_and_others")

            def take_cwt(q):
                act.wait_ge(cwt_ready, q + 1)
                wait(act, base_ready, q)
                act.activation(cwt[:], ps_cwt, ACT.Copy).then_inc(cwt_taken, 1)

            def take_base(q, k):
                act.wait_ge(base_ready, q + 1)
                act.activation(tok[:, k].rearrange("p a b -> p (a b)"), ps_t[0:CT, 0:R * CH], ACT.Copy)\
                   .then_inc(base_taken, 1)

            def gelu(q, b, e):
                n = (2 * q + b) * E + e
                act.wait_ge(hid_ready, n + 1)
                if e == 0:
                    wait(act, out_ready, (2 * q + b - 1) * CHUNKS)
                act.activation(act_h[:, b, e, :], ps_h[:, e % 4, 0:T], ACT.Gelu, bias=col("b1", e)).then_inc(hid_taken, 1)

            def prologue():
                act.preload_act_table_set("natural_log_exp_and_others")
                squares(0)
                inverse_deviation(0)
                squares(1)
                natural_window(0)

            def pair_body(q, k, has_next, has_two, has_before, turn):
                for b in range(2):
                    for e in range(E):
                        gelu(q, b, e)
                        if has_two and (b, e) == (0, 4):
                            squares(q + 2)
                        if has_next and (b, e) == (1, 0):
                            natural_window(q + 1, with_deviation=has_two)
                        if (b, e) == (0, 2):
                            take_cwt(q)
                        if (b, e) == (0, 7):
                            wait(act, stored[k], 2 * 16 * (turn - k))
                            take_base(q, k)

            run_pairs(prologue, pair_body, lambda: None, act)

        @block.vector
        def _(v):
            def normalize(q, k):
                v.wait_ge(rstd_ready, q + 1)
                wait(v, hid_ready, 2 * E * (q - 1))
                v.tensor_tensor(un[:, k, :], cen[:], rstd[:], ALU.mult).then_inc(un_ready, 1)

            def wide(t):
                return t[:].unsqueeze(2).to_broadcast([CT, R, E])

            class Chain:

                def __init__(self, q):
                    self.count = GATE_STEPS * q

                def then(self, ins):
                    ins.then_inc(dve, 1)
                    self.count = self.count + 1
                    v.wait_ge(dve, self.count)

            def shift_logits(q):
                v.wait_ge(logits_ready, q + 1)
                wait(v, exps_ready, q)
                ch = Chain(q)
                ch.then(v.tensor_tensor(lg[:], ps_logits.rearrange("p (a b) -> p a b", a=R), gate_b[0:CT],
                                        ALU.add))
                ch.then(v.tensor_reduce(mx[:], lg[:], AX.X, ALU.max))
                v.tensor_tensor(lg[:], lg[:], wide(mx), ALU.subtract).then_inc(shifted, 1)
                return ch

            def choose(q, k, ch):
                v.wait_ge(exps_ready, q + 1)
                ch.then(v.tensor_reduce(mx[:], pr[:], AX.X, ALU.add))
                ch.then(v.reciprocal(mx[:], mx[:]))
                ch.then(v.tensor_tensor(pr[:], pr[:], wide(mx), ALU.mult))
                ch.then(v.tensor_reduce(mx[:], pr[:], AX.X, ALU.max))
                ch.then(v.tensor_tensor(hit[:], pr[:], wide(mx), ALU.is_equal))
                ch.then(v.tensor_tensor(hit[:], hit[:], rank[0:CT], ALU.mult))
                ch.then(v.tensor_reduce(mx[:], hit[:], AX.X, ALU.max))
                ch.then(v.tensor_tensor(one1[:], hit[:], wide(mx), ALU.is_equal))
                ch.then(v.scalar_tensor_tensor(one2[:], one1[:], -2.0, pr[:], ALU.mult, ALU.add))
                ch.then(v.tensor_reduce(mx[:], one2[:], AX.X, ALU.max))
                ch.then(v.tensor_tensor(hit[:], one2[:], wide(mx), ALU.is_equal))
                ch.then(v.tensor_tensor(hit[:], hit[:], rank[0:CT], ALU.mult))
                ch.then(v.tensor_reduce(mx[:], hit[:], AX.X, ALU.max))
                ch.then(v.tensor_tensor(one2[:], hit[:], wide(mx), ALU.is_equal))
                ch.then(v.tensor_tensor(one1[:], one1[:], one2[:], ALU.add))
                v.tensor_tensor(cw[:, k], pr[:], one1[:], ALU.mult).then_inc(cw_ready, 1)

            def take_chunk(q, k, b, ch):
                n = (2 * q + b) * CHUNKS + ch
                row = b * CHUNKS + ch
                v.wait_ge(out_ready, n + 1)
                v.tensor_tensor(prod[:, row % 2], ps_e[0:CT, row % 2, :].rearrange("p (e n) -> p e n", e=E),
                                cw[:, k, row, :].unsqueeze(2).to_broadcast([CT, E, CH]), ALU.mult).then_inc(out_taken, 1)
                v.wait_ge(out_taken, n + 1)
                v.tensor_reduce(red[:, k, row, :], prod[:, row % 2].rearrange("p e n -> p n e"), AX.X, ALU.add)\
                 .then_inc(reduced, 1)

            def finish(q, k):
                v.wait_ge(reduced, R * (q + 1))
                v.wait_ge(base_taken, q + 1)
                v.tensor_tensor(tok[:, k], tok[:, k], red[:, k], ALU.add).then_inc(finished, 1)

            def prologue():
                normalize(0, 0)
                choose(0, 0, shift_logits(0))

            def pair_body(q, k, has_next, has_two, has_before, turn):
                chain = None
                for b in range(2):
                    for e in range(E):
                        if b or has_before:
                            for ch in AFTER[b].get(e, ()):
                                take_chunk(q if b else q - 1, k if b else 1 - k, 1 - b, ch)
                        if has_before and (b, e) == (0, 7):
                            finish(q - 1, 1 - k)
                        if has_next and (b, e) == (0, 0):
                            normalize(q + 1, 1 - k)
                        if has_next and (b, e) == (0, 4):
                            chain = shift_logits(q + 1)
                        if has_next and (b, e) == (1, 3):
                            choose(q + 1, 1 - k, chain)

            def tail():
                for ch in range(CHUNKS):
                    take_chunk(PAIRS - 1, (PAIRS - 1) % 2, 1, ch)
                finish(PAIRS - 1, (PAIRS - 1) % 2)

            run_pairs(prologue, pair_body, tail, v)

        @block.gpsimd
        def _(g):
            def copy_h(q):
                wait(g, base_ready, q)
                g.tensor_copy(hc[:], h[:, q, :]).then_inc(hc_ready, 1)

            run_pairs(lambda: copy_h(0), lambda q, k, n, n2, b, t: copy_h(q + 1) if n else None, lambda: None, g)


def build(nc, d, out, scratch):
    with ExitStack() as ctx:
        c = load_constants(nc, ctx, d)
        h = ctx.enter_context(nc.sbuf_tensor("h", [P, PAIRS, TOKENS], F32))
        experts = {n: ctx.enter_context(nc.sbuf_tensor("e_" + n, shape, F32)) for n, shape in EXPERT_ARRAYS.items()}
        with ExitStack() as own:
            w = {n: own.enter_context(nc.sbuf_tensor("w_" + n, s, dt)) for n, s, dt in (
                ("decay", [P, 2, 2 * DG * NG], F32), ("wk", [P, 2, 2, DIN], F32), ("skip", [P, 2, P], F32),
                ("wdt", [P, 2, DIN], F32), ("scale", [P, PAIRS], F32), ("shift", [P, PAIRS], F32))}
            token_phase(nc, c, h, w, experts, d)
            mamba_phase(nc, c, h, w, scratch[0], scratch[1])
        expert_phase(nc, c, h, experts, out)


def layouts(np, i):
    f = np.float32
    both = lambda a: np.concatenate([a, a], axis=0)
    arrays = {"x": i["x"].reshape(PAIRS, 2, TOKENS, 2, CH).transpose(0, 1, 4, 3, 2).reshape(PAIRS, P, 2, TOKENS)}
    cols = np.zeros((P, NCOLS), f)

    def put(name, value, k=0):
        value = np.asarray(value)
        value = value.reshape(P, -1)
        at = COLS[name][0] + k
        cols[:, at:at + value.shape[1]] = value

    put("tok_w", both(i["L0_tok_w"].reshape(TAPS, CH).T))
    for name, key in (("tok_b", "L0_tok_b"), ("gamma", "L0_tok_gamma"), ("beta", "L0_tok_beta"), ("alpha", "L0_tok_alpha")):
        put(name, both(i[key]))
    put("b1", i["L0_ffn_b1"].T)
    put("eps_clip", np.full(P, 1e-3, f))
    put("eps_ln", np.full(P, 1e-5, f))
    put("one", np.ones(P, f))
    wx, wz = np.zeros((P, 2, DIN), f), np.zeros((P, 2, DIN), f)
    wo = np.zeros((DIN, 2, 2, P), f)
    wbc, conv_rep = np.zeros((DIN, 2, 2 * NSTATE), f), np.zeros((P, 2, 2, DIN), f)
    xdt, dtw = np.zeros((RANK, 2, DIN), f), np.zeros((RANK, 2, DIN), f)
    for r, n in enumerate("fb"):
        g = lambda name: i[f"L0_attn_{n}_{name}"]
        put("conv_b", g("conv_b"), r)
        put("dt_b", g("dt_b"), r)
        put("D", g("D"), r)
        a = g("A_log").reshape(DG, ND, NG, NN).transpose(3, 1, 0, 2).reshape(P, DG * NG)
        put("a_log", a, r * DG * NG)
        for b in range(2):
            rows = slice(CH * b, CH * b + CH)
            wx[rows, r] = g("in_w")[0:DIN].T
            for two in range(2):
                conv_rep[rows, r, two] = g("conv_w")[:, (2 * b if r == 0 else 2 - 2 * b) + two]
            wo[:, r, b, rows] = g("out_w").T
        wz[0:CH, r] = g("in_w")[DIN:2 * DIN].T
        wbc[:, r] = g("xproj_w")[RANK:].T
        xdt[:, r] = g("xproj_w")[0:RANK]
        dtw[:, r] = g("dt_w").T
    w1, gate_w = np.zeros((P, 2, EXPERTS, HID), f), np.zeros((P, 2, EXPERTS), f)
    rows_of = 2 * CHUNKS
    b2 = np.zeros((rows_of, EXPERTS, rows_of, CH), f)
    for b in range(2):
        rows = slice(CH * b, CH * b + CH)
        w1[rows, b] = i["L0_ffn_W1"].transpose(1, 0, 2)
        gate_w[rows, b] = i["L0_ffn_gate_w"]
    for n in range(rows_of):
        b2[n, :, n] = i["L0_ffn_b2"]
    channel = np.arange(P) // CH
    same = (channel[:, None] == channel[None, :]).astype(f) / f(CH)
    row = np.arange(P)
    d_of, n_of = row % ND, row // ND
    sel_d = np.zeros((P, DG, P), f)
    for g_ in range(DG):
        sel_d[ND * g_ + d_of, g_, row] = 1
    sum_n = np.zeros((P, ND), f)
    sum_n[row, d_of] = 1
    arrays.update(
        cols=cols, ident=np.eye(P, dtype=f), center=np.eye(P, dtype=f) - same, average=same, sel_d=sel_d, sum_n=sum_n,
        wz=wz, wbc=wbc, wo=wo, wx=wx, conv_rep=conv_rep, xdt=xdt, dtw=dtw, w1=w1,
        w2=i["L0_ffn_W2"].transpose(1, 0, 2), b2=b2.reshape(rows_of * EXPERTS, rows_of * CH), gate_w=gate_w,
        gate_b=np.broadcast_to(i["L0_ffn_gate_b"], (P, rows_of, EXPERTS)),
        rank=np.broadcast_to(np.arange(EXPERTS, 0, -1).astype(f), (P, rows_of, EXPERTS)))
    return {n: np.ascontiguousarray(a) for n, a in arrays.items()}


def kernel(**inputs):
    import numpy as np
    import concourse.bacc as bacc
    from concourse.bass_utils import run_bass_kernel_spmd

    nc = bacc.Bacc("TRN2", target_bir_lowering=False, num_devices=1)
    arrays = layouts(np, {n: np.asarray(a) for n, a in inputs.items()})
    d = {n: nc.dram_tensor("in_" + n, a.shape, F32, kind="ExternalInput").ap() for n, a in arrays.items()}
    out = nc.dram_tensor("out", (CLIPS, TOKENS, CH), F32, kind="ExternalOutput").ap()
    scratch = [nc.dram_tensor(n, (2, rows, UNITS, TOKENS), F32, kind="Internal").ap()
               for n, rows in (("bc_scratch", 2 * NSTATE), ("delta_scratch", DIN))]
    build(nc, d, out, scratch)
    r = run_bass_kernel_spmd(nc, [{"in_" + n: a for n, a in arrays.items()}], core_ids=[0])
    return r.results[0]["out"]
```
